# Optimizing a Trainium2 kernel written in Bass

```python
import numpy as np
import jax
import jax.numpy as jnp

def _softmax(x, axis=-1):
    return jax.nn.softmax(x, axis=axis)

def _gelu(x):
    return jax.nn.gelu(x, approximate=True)

def _silu(x):
    return jax.nn.silu(x)

def _sigmoid(x):
    return jax.nn.sigmoid(x)

def _layernorm(x, axis=-1, eps=1e-05):
    m = jnp.mean(x, axis=axis, keepdims=True)
    v = jnp.var(x, axis=axis, keepdims=True)
    return (x - m) / jnp.sqrt(v + eps)

def _scatter_add(tgt, idx, src, axis=0):
    return tgt.at[idx].add(src)

def _segment_sum(src, seg, n):
    return jax.ops.segment_sum(src, seg, n)
kernel_name = 'mk_gnn_preln_d4_gnn_r32_5c0426'

def setup_inputs(seed: int=0):
    np.random.seed(seed)
    _w = jnp.asarray

    def _rec_inputs():
        import jax
        import jax.numpy as jnp
        _gk = jax.random.key(seed)
        x = -0.000202 + 1 * jax.random.normal(jax.random.fold_in(_gk, 1), (3125, 128), jnp.float32)
        src = jax.random.randint(jax.random.fold_in(_gk, 2), (100000,), 0, 3125, jnp.int32)
        dst = jax.random.randint(jax.random.fold_in(_gk, 3), (100000,), 0, 3125, jnp.int32)
        _o = jnp.argsort(dst, stable=True)
        src = src[_o]
        dst = dst[_o]
        return (x, src, dst)
    x, src, dst = _rec_inputs()

    def _L0_gnn_setup():
        import jax, jax.numpy as jnp
        import numpy as np
        N_NODES = 50000
        N_EDGES = 25000
        D_IN = 128
        D_OUT = 128
        key = jax.random.key(seed)
        k1, k2, k3, k4, k5 = jax.random.split(key, 5)
        feature = jax.random.normal(k1, (N_NODES, D_IN), dtype=jnp.float32)
        W = jax.random.normal(k2, (D_OUT, D_IN), dtype=jnp.float32) * (1.0 / np.sqrt(D_IN))
        b = jax.random.normal(k3, (D_OUT,), dtype=jnp.float32) * 0.01
        src = jax.random.randint(k4, (N_EDGES,), 0, N_NODES, dtype=jnp.int32)
        dst = jax.random.randint(k5, (N_EDGES,), 0, N_NODES, dtype=jnp.int32)
        return {'feature': feature, 'W': W, 'b': b, 'src': src, 'dst': dst}
    _L0_gnn_all = _L0_gnn_setup()
    _L0_gnn_in = {k: v for k, v in _L0_gnn_all.items() if k in ('W', 'b')}
    del _L0_gnn_all

    def _L1_gnn_setup():
        import jax, jax.numpy as jnp
        import numpy as np
        NEG_SLOPE = 0.2
        EPS = 1e-16
        N_NODES = 3125
        N_EDGES = 50000
        D = 128
        H = 4
        C = 32
        L = 3

        def _gat_layer(h, src, dst, Ws, Wd, a_s, a_d, bias):
            N = h.shape[0]
            xs = (h @ Ws).reshape(N, H, C)
            xd = (h @ Wd).reshape(N, H, C)
            alpha_s = jnp.sum(xs * a_s, axis=-1)
            alpha_d = jnp.sum(xd * a_d, axis=-1)
            e = alpha_s[src] + alpha_d[dst]
            e = jax.nn.leaky_relu(e, NEG_SLOPE)
            emax = jax.ops.segment_max(e, dst, num_segments=N)
            ex = jnp.exp(e - emax[dst])
            denom = jax.ops.segment_sum(ex, dst, num_segments=N)
            alpha = ex / (denom[dst] + EPS)
            msg = xs[src] * alpha[:, :, None]
            out = jax.ops.segment_sum(msg, dst, num_segments=N)
            return out.reshape(N, H * C) + bias
        key = jax.random.key(seed)
        ks = jax.random.split(key, 7)
        x = jax.random.normal(ks[0], (N_NODES, D), dtype=jnp.float32)
        edge_index = jax.random.randint(ks[1], (2, N_EDGES), 0, N_NODES, dtype=jnp.int32)
        scale = 1.0 / np.sqrt(D)
        Ws = jax.random.normal(ks[2], (L, D, H * C), dtype=jnp.float32) * scale
        Wd = jax.random.normal(ks[3], (L, D, H * C), dtype=jnp.float32) * scale
        att_s = jax.random.normal(ks[4], (L, H, C), dtype=jnp.float32) * scale
        att_d = jax.random.normal(ks[5], (L, H, C), dtype=jnp.float32) * scale
        b = jnp.zeros((L, H * C), dtype=jnp.float32)
        return {'x': x, 'edge_index': edge_index, 'Ws': Ws, 'Wd': Wd, 'att_s': att_s, 'att_d': att_d, 'b': b}
    _L1_gnn_all = _L1_gnn_setup()
    _L1_gnn_in = {k: v for k, v in _L1_gnn_all.items() if k in ('Ws', 'Wd', 'att_s', 'att_d', 'b')}
    del _L1_gnn_all

    def _L2_gnn_setup():
        import jax, jax.numpy as jnp
        import numpy as np
        N, E, D, O = (50000, 25000, 128, 128)
        DELTA = 2.5
        BN_EPS = 1e-05
        key = jax.random.key(seed)
        ks = jax.random.split(key, 8)
        node_feat = jax.random.normal(ks[0], (N, D), dtype=jnp.float32)
        edge_index = jax.random.randint(ks[1], (2, E), 0, N, dtype=jnp.int64)
        M_w = jax.random.normal(ks[2], (D, 2 * D), dtype=jnp.float32) * (1.0 / np.sqrt(2 * D))
        M_b = jnp.zeros((D,), dtype=jnp.float32)
        U_in = (4 * 3 + 1) * D
        U_w = jax.random.normal(ks[3], (O, U_in), dtype=jnp.float32) * (1.0 / np.sqrt(U_in))
        U_b = jnp.zeros((O,), dtype=jnp.float32)
        bn_gamma = jnp.ones((O,), dtype=jnp.float32)
        bn_beta = jnp.zeros((O,), dtype=jnp.float32)
        return {'node_feat': node_feat, 'edge_index': edge_index, 'M_w': M_w, 'M_b': M_b, 'U_w': U_w, 'U_b': U_b, 'bn_gamma': bn_gamma, 'bn_beta': bn_beta}
    _L2_gnn_all = _L2_gnn_setup()
    _L2_gnn_in = {k: v for k, v in _L2_gnn_all.items() if k in ('M_w', 'M_b', 'U_w', 'U_b', 'bn_gamma', 'bn_beta')}
    del _L2_gnn_all

    def _L3_gnn_setup():
        import jax, jax.numpy as jnp
        import numpy as np
        N_NODES = 3125
        N_EDGES = 50000
        D = 128

        def sage_conv_mean(x, src, dst, W_neigh, W_root, b, num_nodes):
            msg = x[src]
            agg = jax.ops.segment_sum(msg, dst, num_segments=num_nodes)
            deg = jax.ops.segment_sum(jnp.ones((src.shape[0],), x.dtype), dst, num_segments=num_nodes)
            agg = agg / jnp.maximum(deg, 1.0)[:, None]
            return agg @ W_neigh + x @ W_root + b
        key = jax.random.key(seed)
        ks = jax.random.split(key, 7)
        s = 1.0 / np.sqrt(D)
        return {'x': jax.random.normal(ks[0], (N_NODES, D), jnp.float32), 'edge_index': jax.random.randint(ks[1], (2, N_EDGES), 0, N_NODES, jnp.int32), 'W1_neigh': jax.random.normal(ks[2], (D, D), jnp.float32) * s, 'W1_root': jax.random.normal(ks[3], (D, D), jnp.float32) * s, 'b1': jnp.zeros((D,), jnp.float32), 'W2_neigh': jax.random.normal(ks[4], (D, D), jnp.float32) * s, 'W2_root': jax.random.normal(ks[5], (D, D), jnp.float32) * s, 'b2': jnp.zeros((D,), jnp.float32)}
    _L3_gnn_all = _L3_gnn_setup()
    _L3_gnn_in = {k: v for k, v in _L3_gnn_all.items() if k in ('W1_neigh', 'W1_root', 'b1', 'W2_neigh', 'W2_root', 'b2')}
    del _L3_gnn_all
    return {'x': x, 'src': src, 'dst': dst, 'L0_gnn_W': _L0_gnn_in['W'], 'L0_gnn_b': _L0_gnn_in['b'], 'L1_gnn_Ws': _L1_gnn_in['Ws'], 'L1_gnn_Wd': _L1_gnn_in['Wd'], 'L1_gnn_att_s': _L1_gnn_in['att_s'], 'L1_gnn_att_d': _L1_gnn_in['att_d'], 'L1_gnn_b': _L1_gnn_in['b'], 'L2_gnn_M_w': _L2_gnn_in['M_w'], 'L2_gnn_M_b': _L2_gnn_in['M_b'], 'L2_gnn_U_w': _L2_gnn_in['U_w'], 'L2_gnn_U_b': _L2_gnn_in['U_b'], 'L2_gnn_bn_gamma': _L2_gnn_in['bn_gamma'], 'L2_gnn_bn_beta': _L2_gnn_in['bn_beta'], 'L3_gnn_W1_neigh': _L3_gnn_in['W1_neigh'], 'L3_gnn_W1_root': _L3_gnn_in['W1_root'], 'L3_gnn_b1': _L3_gnn_in['b1'], 'L3_gnn_W2_neigh': _L3_gnn_in['W2_neigh'], 'L3_gnn_W2_root': _L3_gnn_in['W2_root'], 'L3_gnn_b2': _L3_gnn_in['b2']}

def reference(x, src, dst, L0_gnn_W, L0_gnn_b, L1_gnn_Ws, L1_gnn_Wd, L1_gnn_att_s, L1_gnn_att_d, L1_gnn_b, L2_gnn_M_w, L2_gnn_M_b, L2_gnn_U_w, L2_gnn_U_b, L2_gnn_bn_gamma, L2_gnn_bn_beta, L3_gnn_W1_neigh, L3_gnn_W1_root, L3_gnn_b1, L3_gnn_W2_neigh, L3_gnn_W2_root, L3_gnn_b2):
    import jax
    import jax.numpy as jnp

    def _L0_gnn_ref(feature, W, b, src, dst):
        import jax, jax.numpy as jnp
        import numpy as np
        N_NODES = 50000
        N_EDGES = 25000
        D_IN = 128
        D_OUT = 128
        n = feature.shape[0]
        agg = jax.ops.segment_sum(feature[src], dst, num_segments=n)
        deg = jax.ops.segment_sum(jnp.ones_like(dst, dtype=feature.dtype), dst, num_segments=n)
        mean_h = agg / jnp.maximum(deg, 1.0)[:, None]
        h = jnp.where(deg[:, None] > 0, mean_h, feature)
        return jax.nn.relu(h @ W.T + b)

    def _L1_gnn_ref(x, edge_index, Ws, Wd, att_s, att_d, b):
        import jax, jax.numpy as jnp
        import numpy as np
        NEG_SLOPE = 0.2
        EPS = 1e-16
        N_NODES = 3125
        N_EDGES = 50000
        D = 128
        H = 4
        C = 32
        L = 3

        def _gat_layer(h, src, dst, Ws, Wd, a_s, a_d, bias):
            N = h.shape[0]
            xs = (h @ Ws).reshape(N, H, C)
            xd = (h @ Wd).reshape(N, H, C)
            alpha_s = jnp.sum(xs * a_s, axis=-1)
            alpha_d = jnp.sum(xd * a_d, axis=-1)
            e = alpha_s[src] + alpha_d[dst]
            e = jax.nn.leaky_relu(e, NEG_SLOPE)
            emax = jax.ops.segment_max(e, dst, num_segments=N)
            ex = jnp.exp(e - emax[dst])
            denom = jax.ops.segment_sum(ex, dst, num_segments=N)
            alpha = ex / (denom[dst] + EPS)
            msg = xs[src] * alpha[:, :, None]
            out = jax.ops.segment_sum(msg, dst, num_segments=N)
            return out.reshape(N, H * C) + bias
        src = edge_index[0]
        dst = edge_index[1]
        h = x
        for i in range(L):
            h = _gat_layer(h, src, dst, Ws[i], Wd[i], att_s[i], att_d[i], b[i])
            if i < L - 1:
                h = jax.nn.relu(h)
        return h

    def _L2_gnn_ref(node_feat, edge_index, M_w, M_b, U_w, U_b, bn_gamma, bn_beta):
        import jax, jax.numpy as jnp
        import numpy as np
        N, E, D, O = (50000, 25000, 128, 128)
        DELTA = 2.5
        BN_EPS = 1e-05
        src, dst = (edge_index[0], edge_index[1])
        n = node_feat.shape[0]
        f = jnp.concatenate([node_feat[src], node_feat[dst]], axis=-1)
        msg = f @ M_w.T + M_b
        deg = jax.ops.segment_sum(jnp.ones((msg.shape[0],), msg.dtype), dst, num_segments=n)
        denom = jnp.maximum(deg, 1.0)[:, None]
        ssum = jax.ops.segment_sum(msg, dst, num_segments=n)
        mean = ssum / denom
        has_edge = (deg > 0)[:, None]
        mx = jnp.where(has_edge, jax.ops.segment_max(msg, dst, num_segments=n), 0.0)
        mn = jnp.where(has_edge, jax.ops.segment_min(msg, dst, num_segments=n), 0.0)
        sq_mean = jax.ops.segment_sum(msg * msg, dst, num_segments=n) / denom
        var = jnp.maximum(sq_mean - mean * mean, 0.0)
        std = jnp.sqrt(var + 1e-30)
        h = jnp.concatenate([mean, mx, mn, std], axis=1)
        logd = jnp.log(deg + 1.0)
        amp = (logd / DELTA)[:, None]
        att = (DELTA / (logd + 1e-30))[:, None]
        h = jnp.concatenate([h, h * amp, h * att], axis=1)
        h = jnp.concatenate([node_feat, h], axis=-1) @ U_w.T + U_b
        h = h * jnp.asarray(1.0 / np.sqrt(n), h.dtype)
        mu = jnp.mean(h, axis=0)
        v = jnp.mean((h - mu) ** 2, axis=0)
        h = (h - mu) * jax.lax.rsqrt(v + BN_EPS) * bn_gamma + bn_beta
        return h

    def _L3_gnn_ref(x, edge_index, W1_neigh, W1_root, b1, W2_neigh, W2_root, b2):
        import jax, jax.numpy as jnp
        import numpy as np
        N_NODES = 3125
        N_EDGES = 50000
        D = 128

        def sage_conv_mean(x, src, dst, W_neigh, W_root, b, num_nodes):
            msg = x[src]
            agg = jax.ops.segment_sum(msg, dst, num_segments=num_nodes)
            deg = jax.ops.segment_sum(jnp.ones((src.shape[0],), x.dtype), dst, num_segments=num_nodes)
            agg = agg / jnp.maximum(deg, 1.0)[:, None]
            return agg @ W_neigh + x @ W_root + b
        src, dst = (edge_index[0], edge_index[1])
        n = x.shape[0]
        h = sage_conv_mean(x, src, dst, W1_neigh, W1_root, b1, n)
        h = jax.nn.relu(h)
        h = sage_conv_mean(h, src, dst, W2_neigh, W2_root, b2, n)
        return h
    edge_index = jnp.stack([src, dst])
    h = jnp.maximum(_layernorm(x, axis=-1), 0.0)
    x = x + _L0_gnn_ref(h, L0_gnn_W, L0_gnn_b, src, dst)
    h = jnp.maximum(_layernorm(x, axis=-1), 0.0)
    x = x + _L1_gnn_ref(h, edge_index, L1_gnn_Ws, L1_gnn_Wd, L1_gnn_att_s, L1_gnn_att_d, L1_gnn_b)
    h = jnp.maximum(_layernorm(x, axis=-1), 0.0)
    x = x + _L2_gnn_ref(h, edge_index, L2_gnn_M_w, L2_gnn_M_b, L2_gnn_U_w, L2_gnn_U_b, L2_gnn_bn_gamma, L2_gnn_bn_beta)
    h = jnp.maximum(_layernorm(x, axis=-1), 0.0)
    x = x + _L3_gnn_ref(h, edge_index, L3_gnn_W1_neigh, L3_gnn_W1_root, L3_gnn_b1, L3_gnn_W2_neigh, L3_gnn_W2_root, L3_gnn_b2)
    return x

_drawn_inputs = setup_inputs


def setup_inputs(seed=0):
    import zlib

    import numpy as np

    out = dict(_drawn_inputs(seed))
    spreads = {'L1_gnn_b': (0.0, 0.1),
     'L2_gnn_M_b': (0.0, 0.8),
     'L2_gnn_U_b': (0.0, 0.8),
     'L2_gnn_bn_gamma': (1.0, 0.2),
     'L2_gnn_bn_beta': (0.0, 0.1),
     'L3_gnn_b1': (0.0, 0.1),
     'L3_gnn_b2': (0.0, 0.1)}
    factors = {'L0_gnn_b': 8.0, 'L1_gnn_Wd': 8.0, 'L1_gnn_att_s': 7.516, 'L1_gnn_att_d': 8.0}
    for name, (base, spread) in spreads.items():
        noise = np.random.default_rng([zlib.crc32(name.encode()), seed]).standard_normal(out[name].shape)
        drawn = base * np.exp(spread * noise) if base else spread * noise
        out[name] = jnp.asarray(drawn.astype(out[name].dtype))
    for name, factor in factors.items():
        out[name] = (out[name] * factor).astype(out[name].dtype)
    return out
```

```python
from contextlib import ExitStack

import concourse.bass as bass
from concourse import mybir

ALU = mybir.AluOpType
ACT = mybir.ActivationFunctionType
F32 = mybir.dt.float32
BF16 = mybir.dt.bfloat16
I32 = mybir.dt.int32

P = 128
D = 128
H = 4
C = D // H
HC = C + 1
GATW = H * HC
BIG = 1.5e38
NEG_SLOPE, GAT_EPS = 0.2, 1e-16
LN_EPS, BN_EPS, STD_EPS, PNA_DELTA = 1e-5, 1e-5, 1e-30, 2.5

MEAN0, GAT, PNA, MEAN1, MEAN2 = "mean0", "gat", "pna", "mean1", "mean2"
KINDS = [MEAN0, GAT, GAT, GAT, PNA, MEAN1, MEAN2]
GAT_FIRST, PNA_PASS, OUT_PASS = 1, 4, 6
NORMED = [0, 1, 4, 5]
SLOTS = 4
ROWS_SLOTS = 2


class Pass:

    def __init__(self, number, kind, lane, before):
        self.number, self.kind = number, kind
        self.steps = 7 if kind == PNA else 14
        self.groups = lane // self.steps
        self.rounds = self.groups // SLOTS
        self.table_w = H * HC + 2 * H if kind == GAT else D
        self.step_w = {PNA: 3 * D, GAT: self.table_w}.get(kind, D)
        self.gather_at = D if kind == PNA else 0
        self.state_w = {PNA: 4 * D, GAT: GATW + H}.get(kind, D)
        self.ops = 1 if kind in (MEAN0, MEAN1, MEAN2) else 2
        self.updates = self.groups * self.steps * self.ops
        b = before
        self.gathers0 = b.gathers0 + b.rounds * b.steps * 16 if b else 0
        self.groups0 = b.groups0 + b.groups if b else 0
        self.steps0 = (b.steps0 + b.updates if b else 0) + 1
        self.rows0 = b.rows0 + b.groups // ROWS_SLOTS * 16 if b else 0
        self.small0 = b.small0 + (12 * b.groups if b.kind == GAT else 0) if b else 0
        self.exps0 = b.exps0 + (b.groups if b.kind == GAT else 0) if b else 0

    def gathered(self, rnd):
        return self.gathers0 + self.steps * 16 + rnd * (self.steps * 16)

    def updated(self, rnd, s):
        n = self.steps * self.ops
        return rnd * (SLOTS * n) + (self.steps0 + (s + 1) * n)


def build(nc, x, src, dst, W0, b0, Ws, Wd, att_s, att_d, gat_b, M_w, M_b, U_w, U_b, gamma, beta,
          W1n, W1r, b1, W2n, W2r, b2, out):
    N, E = x.shape[0], src.shape[0]
    NT = 25
    NP = N // NT
    NN = P * NT
    LANE = 784
    EP = P * LANE
    LAST_LANE = E - (P - 1) * LANE
    HI = NN // P
    assert N == NP * NT and NP <= P and 0 < LAST_LANE <= LANE and LANE % (14 * SLOTS) == 0

    passes = []
    for n, kind in enumerate(KINDS):
        passes.append(Pass(n, kind, LANE, passes[-1] if passes else None))
    GMAX = max(SLOTS * p.steps * p.step_w for p in passes)
    RMAX = max(ROWS_SLOTS * p.steps * p.state_w for p in passes)
    TW = max(p.table_w for p in passes)

    with ExitStack() as ctx:
        def sb(name, shape, dt=F32):
            return ctx.enter_context(nc.sbuf_tensor(name, shape, dt))

        def ps(name, shape):
            return ctx.enter_context(nc.psum_tensor(name, shape, F32))

        def sem(name):
            return ctx.enter_context(nc.semaphore(name))

        table_d = {w: nc.dram_tensor(f"table{w}", (NN, w), F32).ap() for w in {p.table_w for p in passes}}
        rows_d = {w: nc.dram_tensor(f"rows{w}", (EP, w), F32).ap() for w in {p.state_w for p in passes}}
        start_ad_d = nc.dram_tensor("start_ad", (EP + NN, H), F32).ap()
        degree_d = nc.dram_tensor("degree", (NN,), F32).ap()
        start_d = nc.dram_tensor("start", (NN,), F32).ap()
        last_d = nc.dram_tensor("last", (NN,), F32).ap()

        xt = sb("xt", [P, NT, D])
        hT = sb("hT", [P, NT, P])
        root = sb("root", [P, NT, D])
        ring = sb("ring", [P, GMAX + RMAX])
        side = sb("side", [P, max(LANE * H, NT * (GATW + H))])
        pick = sb("pick", [P, NN])
        src_i = sb("src_i", [P, LANE], I32)
        dst_i = sb("dst_i", [P, LANE], I32)
        lo_hi = sb("lo_hi", [P, 2, LANE])
        keep = sb("keep", [P, 2, LANE])
        fresh = sb("fresh", [P, LANE])
        src_win = sb("src_win", [P, SLOTS, 14], I32)
        keep_win = sb("keep_win", [P, SLOTS, 2, 14])
        onehot = sb("onehot", [P, 2, 14, P + HI], BF16)
        iota_lo = sb("iota_lo", [P, P])
        zeros_b = sb("zeros_b", [P, P], BF16)
        ident = sb("ident", [P, P])
        ones = sb("ones", [P, P])
        before = sb("before", [P, P])
        lane_last = sb("lane_last", [P, 2])
        node_id = sb("node_id", [P, NT])
        same = sb("same", [P, 2, P])
        dlast = sb("dlast", [P, 2, P])
        dfirst_i = sb("dfirst_i", [P, 1], I32)
        hist = sb("hist", [HI, P])
        deg = sb("deg", [P, NT])
        tmp = sb("tmp", [P, 4, NT])
        start = sb("start_s", [P, NT])
        last = sb("last_s", [P, NT])
        has = sb("has", [P, NT])
        nohas = sb("nohas", [P, NT])
        hrec = sb("hrec", [P, NT])
        cbias = sb("cbias", [P, NT])
        amp = sb("amp", [P, NT])
        att = sb("att", [P, NT])
        end_i = sb("end_i", [P, NT], I32)
        start_i = sb("start_i", [P, NT], I32)
        stats = sb("stats", [P, NT, 6])
        mv = sb("mv", [P, NT, 2])
        rstd = sb("rstd", [P, NT])
        wT = sb("wT", [P, 16, D])
        w_att = sb("w_att", [P, 3, GATW + H])
        w_sage = sb("w_sage", [P, 2, 2 * D])
        rowb = sb("rowb", [P, 10, D])
        B0, BG, BM, BU, BGAM, BBET, B1, B2 = 0, 1, 4, 5, 6, 7, 8, 9
        eps = sb("eps", [P, 2])
        e_b = sb("e_b", [P, 14, H])
        m_b = sb("m_b", [P, 15, H])
        d_b = sb("d_b", [P, 2, 14, H])
        cw_b = sb("cw_b", [P, 2, 14, H])
        ad_first = sb("ad_first", [P, TW])
        lane_x = sb("lane_x", [P, 4, P])
        lane_s = sb("lane_s", [P, 4, P])
        lane_e = sb("lane_e", [P, 2, P])
        Z = sb("Z", [P, 4 * D])
        sm = sb("sm", [P, 3, NT, 2 * H])
        rden = sb("rden", [P, NT, H])
        aggT = sb("aggT", [P, 2, 4 * P])
        bn = sb("bn", [P, 3, D])

        psT = [ps(f"psT{i}", [P, 512]) for i in range(2)]
        psY = [ps(f"psY{i}", [P, 512]) for i in range(2)]
        psL = ps("psL", [P, 512])
        psZ = ps("psZ", [P, 512])
        psH = ps("psH", [P, 512])
        psS = ps("psS", [P, 512])

        assert 25 * D == NT * D
        flat = root[:].rearrange("p t d -> p (t d)")
        w_raw = flat[:, 0:16 * D].rearrange("p (k d) -> p k d", d=D)
        w_d = flat[:, 16 * D:19 * D].rearrange("p (l d) -> p l d", d=D)
        att_sb = flat[:, 19 * D:25 * D].rearrange("p (a l d) -> p a l d", l=3, d=D)
        part_i = ring[:, 0:LANE].bitcast(I32)

        def gathered_rows(p, s):
            n = p.steps * p.step_w
            return ring[:, s * n:(s + 1) * n].rearrange("p (k w) -> p k w", w=p.step_w)

        def state_rows(p, r):
            n = p.steps * p.state_w
            return ring[:, GMAX + r * n:GMAX + (r + 1) * n].rearrange("p (k w) -> p k w", w=p.state_w)

        def ytab(p):
            return ring[:, 0:NT * p.table_w].rearrange("p (t w) -> p t w", w=p.table_w)

        u = ring[:, NT * TW:NT * (TW + D)].rearrange("p (t w) -> p t w", w=D)
        bc_start = ring[:, 3400:3400 + NN]
        bc_last = ring[:, 3400 + NN:3400 + 2 * NN]
        assert 3400 + 2 * NN <= GMAX

        def ends(p):
            return ring[:, 0:NT * p.state_w].rearrange("p (t w) -> p t w", w=p.state_w)

        def pick_t(t):
            return pick[:].rearrange("q (p t) -> q t p", t=NT)[:, t, :]

        ad_lane = side[:, 0:LANE * H].rearrange("p (j h) -> p j h", h=H)
        crossed = side[:, 0:NT * (GATW + H)].rearrange("p (t w) -> p t w", w=GATW + H)
        hbn = side[:, 0:NT * D].rearrange("p (t w) -> p t w", w=D)

        cleared = sem("cleared")
        src_in, dst_in, x_in = sem("src_in"), sem("dst_in"), sem("x_in")
        w_in = sem("w_in")
        zero_in = sem("zero_in")
        const_rdy = sem("const_rdy")
        const_step = sem("const_step")
        wT_ps, wT_rdy = sem("wT_ps"), sem("wT_rdy")
        dl_ps = sem("dl_ps")
        dve_chain = sem("dve_chain")
        dl_rdy = sem("dl_rdy")
        lanes_rdy = sem("lanes_rdy")
        var_rdy, std_rdy = sem("var_rdy"), sem("std_rdy")
        u_rdy = sem("u_rdy")
        hT_ps, hT_rdy = sem("hT_ps"), sem("hT_rdy")
        y_ps, y_rdy = sem("y_ps"), sem("y_rdy")
        table_out = sem("table_out")
        ad_scattered = sem("ad_scattered")
        ad_in, ad_first_in = sem("ad_in"), sem("ad_first_in")
        gathered = [sem(f"gathered{s}") for s in range(SLOTS)]
        gate = sem("gate")
        src_rdy, keep_rdy = sem("src_rdy"), sem("keep_rdy")
        updated = sem("updated")
        small = sem("small")
        exp_in, exp_rdy = sem("exp_in"), sem("exp_rdy")
        sq_rdy = sem("sq_rdy")
        rows_out = [sem(f"rows_out{r}") for r in range(ROWS_SLOTS)]
        onehot_rdy, counted = sem("onehot_rdy"), sem("counted")
        hist_rdy, hist_out, deg_in = sem("hist_rdy"), sem("hist_out"), sem("deg_in")
        sums_rdy, base_ps = sem("sums_rdy"), sem("base_ps")
        seg_rdy, seg_out, seg_in = sem("seg_rdy"), sem("seg_out"), sem("seg_in")
        index_rdy = sem("index_rdy")
        pick_rdy, cross_ps = sem("pick_rdy"), sem("cross_ps")
        laneL_rdy = sem("laneL_rdy")
        laneT_ps = sem("laneT_ps")
        laneE_in, laneE_rdy = sem("laneE_in"), sem("laneE_rdy")
        laneS_rdy = sem("laneS_rdy")
        laneZ_ps, Z_rdy = sem("laneZ_ps"), sem("Z_rdy")
        node_ps, node_rdy = sem("node_ps"), sem("node_rdy")
        ends_in = sem("ends_in")
        ga_in, ga_rdy = sem("ga_in"), sem("ga_rdy")
        ln_in, ln_rdy = sem("ln_in"), sem("ln_rdy")
        sd_in, sd_rdy = sem("sd_in"), sem("sd_rdy")
        agg_rdy = sem("agg_rdy")
        aggT_ps, aggT_rdy = sem("aggT_ps"), sem("aggT_rdy")
        pna_ps, pna_rdy = sem("pna_ps"), sem("pna_rdy")
        bn_in, bn_ps, bn_sq_in, bn_sq = sem("bn_in"), sem("bn_ps"), sem("bn_sq_in"), sem("bn_sq")
        bn_var, bn_std = sem("bn_var"), sem("bn_std")
        done, stored = sem("done"), sem("stored")

        loads = [(w_raw[:, 0, :], W0), (w_raw[:, 1, :], M_w[:, 0:D]), (w_raw[:, 2, :], M_w[:, D:2 * D]),
                 (w_raw[:, 3:16, :], U_w.rearrange("o (k d) -> o k d", d=D)),
                 (w_att[:, :, 0:D], Ws.rearrange("l k n -> k l n")),
                 (w_d, Wd.rearrange("l k n -> k l n")),
                 (att_sb[:, 0, :, :], att_s.rearrange("l h c -> l (h c)").partition_broadcast(P)),
                 (att_sb[:, 1, :, :], att_d.rearrange("l h c -> l (h c)").partition_broadcast(P)),
                 (w_sage[:, 0, 0:D], W1n), (w_sage[:, 0, D:2 * D], W1r),
                 (w_sage[:, 1, 0:D], W2n), (w_sage[:, 1, D:2 * D], W2r),
                 (rowb[:, BG:BG + 3, :], gat_b.partition_broadcast(P))]
        loads += [(rowb[:, n, :], v.partition_broadcast(P))
                  for n, v in ((B0, b0), (BM, M_b), (BU, U_b), (BGAM, gamma), (BBET, beta), (B1, b1), (B2, b2))]

        block = ctx.enter_context(nc.Block())

        @block.sync
        def _(sp):
            sp.wait_ge(cleared, 1)
            sp.dma_start(dst_i[0:P - 1, :], dst[0:(P - 1) * LANE].rearrange("(p j) -> p j", j=LANE)).then_inc(dst_in, 16)
            sp.dma_start(dst_i[P - 1:P, 0:LAST_LANE],
                         dst[(P - 1) * LANE:E].rearrange("(a j) -> a j", a=1)).then_inc(dst_in, 16)
            sp.wait_ge(cleared, 2)
            sp.dma_start(src_i[0:P - 1, :], src[0:(P - 1) * LANE].rearrange("(p j) -> p j", j=LANE)).then_inc(src_in, 16)
            sp.dma_start(src_i[P - 1:P, 0:LAST_LANE],
                         src[(P - 1) * LANE:E].rearrange("(a j) -> a j", a=1)).then_inc(src_in, 16)
            sp.wait_ge(cleared, 3)
            sp.dma_start(xt[0:NP, :, :], x.rearrange("(p t) d -> p t d", t=NT)).then_inc(x_in, 16)
            for to, frm in loads:
                sp.dma_start(to, frm).then_inc(w_in, 16)
            sp.wait_ge(cleared, 4)
            sp.dma_start(start_ad_d[0:EP, :].rearrange("(p j) h -> p (j h)", p=P),
                         side[:, 0:LANE * H]).then_inc(zero_in, 16)

            for p in passes:
                sp.wait_ge(y_rdy, 2 * NT * (p.number + 1))
                sp.dma_start(table_d[p.table_w].rearrange("(p t) w -> p t w", t=NT), ytab(p)).then_inc(table_out, 16)
                if p.kind == GAT:
                    sp.wait_ge(ad_scattered, 16 * NT * (p.number - GAT_FIRST + 1))
                    sp.dma_start(ad_lane, start_ad_d[0:EP, :].rearrange("(p j) h -> p j h", p=P)).then_inc(ad_in, 16)
                lanes = rows_d[p.state_w].rearrange("(p j) w -> p j w", j=LANE)

                def store(rnd):
                    for s in range(SLOTS):
                        sp.wait_ge(updated, p.updated(rnd, s))
                        sp.dma_start(lanes[:, bass.ds(rnd * (SLOTS * p.steps) + s * p.steps, p.steps), :],
                                     state_rows(p, s % ROWS_SLOTS)).then_inc(rows_out[s % ROWS_SLOTS], 16)

                with sp.Fori(0, p.rounds, 1) as rnd:
                    store(rnd)
                if p.number == 0:
                    sp.wait_ge(hist_rdy, 1)
                    sp.dma_start(degree_d.rearrange("(a b) -> a b", b=P), hist[:]).then_inc(hist_out, 16)
                    sp.wait_ge(hist_out, 16)
                    sp.dma_start(deg[:], degree_d.rearrange("(p t) -> p t", t=NT)).then_inc(deg_in, 16)
                    sp.wait_ge(seg_rdy, 2)
                    sp.dma_start(start_d.rearrange("(p t) -> p t", t=NT), start[:]).then_inc(seg_out, 16)
                    sp.dma_start(last_d.rearrange("(p t) -> p t", t=NT), last[:]).then_inc(seg_out, 16)
                    sp.wait_ge(seg_out, 32)
                    sp.dma_start(bc_start, start_d.partition_broadcast(P)).then_inc(seg_in, 16)
                    sp.dma_start(bc_last, last_d.partition_broadcast(P)).then_inc(seg_in, 16)
            sp.wait_ge(done, 1)
            sp.dma_start(out.rearrange("(p t) d -> p t d", t=NT), xt[0:NP, :, :]).then_inc(stored, 16)
            sp.wait_ge(stored, 16)
            sp.wait_ge(zero_in, 16)
            sp.wait_ge(table_out, 16 * len(passes))
            for r in range(ROWS_SLOTS):
                sp.wait_ge(rows_out[r], passes[-1].rows0 + passes[-1].groups // ROWS_SLOTS * 16)

        @block.gpsimd
        def _(pool):
            pool.memset(ident[:], 0.0).then_inc(const_step, 1)
            pool.memset(before[:], 0.0).then_inc(const_step, 1)
            pool.wait_ge(const_step, 2)
            pool.affine_select(out=ident[:], in_=ident[:], compare_op=ALU.not_equal, fill=1.0, base=0,
                               pattern=[[-1, P]], channel_multiplier=1).then_inc(const_rdy, 1)
            pool.affine_select(out=before[:], in_=before[:], compare_op=ALU.is_ge, fill=1.0, base=0,
                               pattern=[[-1, P]], channel_multiplier=1).then_inc(const_rdy, 1)
            pool.iota(iota_lo[:], [[1, P]], base=0, channel_multiplier=0,
                      allow_small_or_imprecise_dtypes=True).then_inc(const_rdy, 1)
            pool.iota(lane_last[:], [[LANE, 2]], base=LANE - 1, channel_multiplier=LANE,
                      allow_small_or_imprecise_dtypes=True).then_inc(const_rdy, 1)
            pool.iota(node_id[:], [[1, NT]], base=0, channel_multiplier=NT,
                      allow_small_or_imprecise_dtypes=True).then_inc(const_rdy, 1)

            for p in passes:
                g = p.number - GAT_FIRST
                if p.kind == GAT:
                    pool.wait_ge(y_rdy, 2 * NT * (p.number + 1))
                    pool.wait_ge(zero_in, 16)
                    if g:
                        pool.wait_ge(ad_in, 16 * g)
                    for t in range(NT):
                        pool.indirect_dma_start(out=start_ad_d, out_offset=bass.IndirectOffsetOnAxis(
                            ap=start_i[:, t:t + 1], axis=0), in_=ytab(p)[:, t, GATW + H:GATW + 2 * H],
                            in_offset=None).then_inc(ad_scattered, 16)
                pool.wait_ge(table_out, 16 * (p.number + 1))
                table = table_d[p.table_w]
                if p.kind == GAT:
                    pool.indirect_dma_start(out=ad_first[:, 0:p.table_w], out_offset=None, in_=table,
                                            in_offset=bass.IndirectOffsetOnAxis(ap=dfirst_i[:, 0:1], axis=0)
                                            ).then_inc(ad_first_in, 16)
                    pool.wait_ge(ad_scattered, 16 * NT * (g + 1))

                def gather(rnd):
                    for s in range(SLOTS):
                        pool.wait_ge(src_rdy, rnd * SLOTS + (p.groups0 + s + 1))
                        if type(rnd) is not int:
                            pool.sem_inc(gate, 1)
                        if type(rnd) is not int or rnd > 0:
                            pool.wait_ge(updated, p.updated(rnd - 1, s))
                            if type(rnd) is not int:
                                pool.sem_inc(gate, 1)
                        rows = gathered_rows(p, s)
                        for k in range(p.steps):
                            pool.indirect_dma_start(
                                out=rows[:, k, p.gather_at:p.gather_at + p.table_w], out_offset=None, in_=table,
                                in_offset=bass.IndirectOffsetOnAxis(ap=src_win[:, s, k:k + 1], axis=0)
                            ).then_inc(gathered[s], 16)

                gather(0)
                with pool.Fori(1, p.rounds, 1) as rnd:
                    gather(rnd)

                pool.wait_ge(index_rdy, 2)
                for r in range(ROWS_SLOTS):
                    pool.wait_ge(rows_out[r], p.rows0 + p.groups // ROWS_SLOTS * 16)
                pool.wait_ge(laneT_ps, p.number + 1)
                for t in range(NT):
                    pool.indirect_dma_start(out=ends(p)[:, t, :], out_offset=None, in_=rows_d[p.state_w],
                                            in_offset=bass.IndirectOffsetOnAxis(ap=end_i[:, t:t + 1], axis=0)
                                            ).then_inc(ends_in, 16)

        @block.scalar
        def _(act):
            norm = 0
            act.wait_ge(src_in, 32)
            act.wait_ge(lanes_rdy, 1)
            for p in passes:
                if p.number in NORMED:
                    norm += 1
                    act.wait_ge(var_rdy, norm)
                    nc.scalar.activation(rstd[:], mv[:, :, 1], ACT.Sqrt, bias=eps[:, 0:1]).then_inc(std_rdy, 1)
                for b in range(7):
                    k = min(4, NT - 4 * b)
                    act.wait_ge(hT_ps, 7 * p.number + b + 1)
                    nc.scalar.activation(hT[:, 4 * b:4 * b + k, :],
                                         psT[b % 2][:, 0:k * P].rearrange("f (t n) -> f t n", n=P),
                                         ACT.Relu).then_inc(hT_rdy, 1)

                def window(rnd, s):
                    at = bass.ds(rnd * (SLOTS * p.steps) + s * p.steps, p.steps)
                    z = s % SLOTS
                    nc.scalar.copy(src_win[:, z, 0:p.steps], src_i[:, at]).then_inc(src_rdy, 1)
                    nc.scalar.copy(keep_win[:, z, :, 0:p.steps], keep[:, :, at]).then_inc(keep_rdy, 1)

                def group(rnd, s, final):
                    if not (final and s >= SLOTS - 2):
                        if type(rnd) is not int or rnd > 0 or s >= 2:
                            act.wait_ge(gathered[(s - 2) % SLOTS], p.gathered(rnd if s >= 2 else rnd - 1))
                            act.wait_ge(updated, p.updated(rnd, s - 2))
                        window(rnd, s + 2)
                    if p.kind == GAT:
                        act.wait_ge(small, rnd * (12 * SLOTS) + (p.small0 + 12 * s + 9))
                        nc.scalar.activation(cw_b[:], d_b[:], ACT.Exp).then_inc(exp_rdy, 1)
                    if p.kind == PNA:
                        rows = gathered_rows(p, s)
                        act.wait_ge(gathered[s], p.gathered(rnd))
                        nc.scalar.activation(rows[:, :, 0:D], rows[:, :, D:2 * D], ACT.Square).then_inc(sq_rdy, 1)
                        nc.scalar.mul(rows[:, :, 2 * D:3 * D], rows[:, :, D:2 * D], -1.0).then_inc(sq_rdy, 1)

                if p.number:
                    act.wait_ge(updated, p.steps0 - 1)
                window(0, 0)
                window(0, 1)
                for s in range(SLOTS):
                    group(0, s, False)
                with act.Fori(1, p.rounds - 1, 1) as rnd:
                    for s in range(SLOTS):
                        group(rnd, s, False)
                for s in range(SLOTS):
                    group(p.rounds - 1, s, True)

                if p.number == 0:
                    act.wait_ge(ln_in, 1)
                    nc.scalar.activation(amp[:], deg[:], ACT.Ln, bias=1.0).then_inc(ln_rdy, 1)
                if p.kind == GAT:
                    g = p.number - GAT_FIRST
                    act.wait_ge(laneE_in, g + 1)
                    nc.scalar.activation(lane_e[:], lane_e[:], ACT.Exp).then_inc(laneE_rdy, 1)
                    act.wait_ge(ga_in, g + 1)
                    nc.scalar.activation(sm[:, 1, :, :], sm[:, 1, :, :], ACT.Exp).then_inc(ga_rdy, 1)
                if p.kind == PNA:
                    act.wait_ge(sd_in, 1)
                    nc.scalar.activation(ends(p)[:, :, 0:D], ends(p)[:, :, 0:D], ACT.Sqrt,
                                         bias=eps[:, 1:2]).then_inc(sd_rdy, 1)
                    for t in range(NT):
                        act.wait_ge(aggT_ps, t + 1)
                        if t >= 2:
                            act.wait_ge(pna_ps, t - 1)
                        nc.scalar.copy(aggT[:, t % 2, :], psT[t % 2][:]).then_inc(aggT_rdy, 1)
                    act.wait_ge(bn_var, 1)
                    nc.scalar.activation(bn[:, 2, :], bn[:, 1, :], ACT.Sqrt, bias=eps[:, 0:1]).then_inc(bn_std, 1)

        @block.tensor
        def _(pe):
            pe.wait_ge(const_rdy, 5)
            pe.wait_ge(w_in, 16 * len(loads))
            for b in range(4):
                if b >= 2:
                    pe.wait_ge(wT_rdy, b - 1)
                for k in range(4):
                    ins = nc.tensor.transpose(psT[b % 2][:, k * P:(k + 1) * P], w_raw[:, 4 * b + k, :], ident[:])
                ins.then_inc(wT_ps, 1)
            pe.wait_ge(dl_rdy, 1)
            nc.tensor.transpose(psL[:, 0:P], dlast[:, 0, :], ident[:]).then_inc(dl_ps, 1)
            pe.wait_ge(wT_rdy, 4)

            for p in passes:
                g = p.number - GAT_FIRST
                pe.wait_ge(u_rdy, p.number + 1)
                for b in range(7):
                    if b >= 2:
                        pe.wait_ge(hT_rdy, 7 * p.number + b - 1)
                    for t in range(4 * b, min(4 * b + 4, NT)):
                        ins = nc.tensor.transpose(psT[b % 2][:, (t % 4) * P:(t % 4 + 1) * P], u[:, t, :], ident[:])
                    ins.then_inc(hT_ps, 1)
                w = {MEAN0: wT[:, 0, :], GAT: w_att[:, g % 3, :], PNA: wT[:, 1:3, :].rearrange("p a d -> p (a d)"),
                     MEAN1: w_sage[:, 0, :], MEAN2: w_sage[:, 1, :]}[p.kind]
                for t in range(NT):
                    pe.wait_ge(hT_rdy, 7 * p.number + t // 4 + 1)
                    if t >= 2:
                        pe.wait_ge(y_rdy, 2 * NT * p.number + 2 * (t - 1))
                    nc.tensor.matmul(psY[t % 2][:, 0:w.shape[1]], hT[:, t, :], w, start=True, stop=True).then_inc(y_ps, 1)

                if p.number == 0:
                    pe.wait_ge(cleared, 5)
                    nc.tensor.matmul(psH[0:HI, 0:P], zeros_b[:, 0:HI], zeros_b[:], start=True, stop=False,
                                     skip_group_check=True)

                    def count(rnd):
                        for s in range(SLOTS):
                            pe.wait_ge(onehot_rdy, rnd * (2 * SLOTS) + 2 * (s + 1))
                            for k in range(p.steps):
                                ins = nc.tensor.matmul(psH[0:HI, 0:P], onehot[:, s % 2, k, P:P + HI],
                                                       onehot[:, s % 2, k, 0:P], start=False, stop=False,
                                                       skip_group_check=True)
                            ins.then_inc(counted, 1)

                    with pe.Fori(0, p.rounds, 1) as rnd:
                        count(rnd)
                    nc.tensor.matmul(psH[0:HI, 0:P], zeros_b[:, 0:HI], zeros_b[:], start=False, stop=True,
                                     skip_group_check=True).then_inc(counted, 1)
                    pe.wait_ge(sums_rdy, 1)
                    nc.tensor.matmul(psS[:, 0:1], before[:], tmp[:, 0, NT - 1:NT], start=True, stop=True).then_inc(base_ps, 1)
                    pe.wait_ge(pick_rdy, 1)
                    for t in range(NT):
                        ins = nc.tensor.matmul(psS[:, 32 + t:33 + t], pick_t(t), ones[:, 0:1], start=True, stop=True)
                    ins.then_inc(cross_ps, 1)

                parts = {GAT: 3, PNA: 4}.get(p.kind, 1)
                if p.kind == GAT:
                    pe.wait_ge(laneL_rdy, 3 * (g + 1))
                else:
                    pe.wait_ge(updated, p.updated(p.rounds - 1, SLOTS - 1))
                for k in range(parts):
                    frm = lane_x[:, k, :] if p.kind == GAT else state_rows(p, 1)[:, p.steps - 1, k * D:(k + 1) * D]
                    ins = nc.tensor.transpose(psL[:, k * P:(k + 1) * P], frm, ident[:])
                ins.then_inc(laneT_ps, 1)
                pe.wait_ge(laneS_rdy, p.number + 1)
                for k in range(parts):
                    ins = nc.tensor.transpose(psZ[:, k * P:(k + 1) * P], lane_s[:, k, :], ident[:])
                ins.then_inc(laneZ_ps, 1)
                pe.wait_ge(Z_rdy, p.number + 1)
                for t in range(NT):
                    if t >= 2:
                        pe.wait_ge(node_rdy, NT * p.number + t - 1)
                    nc.tensor.matmul(psY[t % 2][:, 0:p.state_w], pick_t(t), Z[:, 0:p.state_w],
                                     start=True, stop=True).then_inc(node_ps, 1)

                if p.kind == PNA:
                    pe.wait_ge(agg_rdy, 1)
                    for t in range(NT + 1):
                        if t < NT:
                            if t >= 2:
                                pe.wait_ge(aggT_rdy, t - 1)
                            for k in range(4):
                                ins = nc.tensor.transpose(psT[t % 2][:, k * P:(k + 1) * P],
                                                          ends(p)[:, t, k * D:(k + 1) * D], ident[:])
                            ins.then_inc(aggT_ps, 1)
                        if t >= 1:
                            v = t - 1
                            if v >= 2:
                                pe.wait_ge(pna_rdy, v - 1)
                            nc.tensor.matmul(psY[v % 2][:, 3 * D:4 * D], hT[:, v, :], wT[:, 3, :], start=True, stop=True)
                            pe.wait_ge(aggT_rdy, v + 1)
                            for k, c in enumerate((3, 0, 1, 2)):
                                for f in range(3):
                                    ins = nc.tensor.matmul(psY[v % 2][:, f * D:(f + 1) * D],
                                                           aggT[:, v % 2, k * P:(k + 1) * P], wT[:, 4 + 4 * f + c, :],
                                                           start=(k == 0 and f == 0), stop=(k == 3 and f == 2),
                                                           skip_group_check=True)
                            ins.then_inc(pna_ps, 1)
                    pe.wait_ge(bn_in, 1)
                    for t in range(NT):
                        ins = nc.tensor.matmul(psS[:, 0:D], ones[0:NP, :], hbn[0:NP, t, :], start=(t == 0), stop=(t == NT - 1))
                    ins.then_inc(bn_ps, 1)
                    pe.wait_ge(bn_sq_in, 1)
                    for t in range(NT):
                        ins = nc.tensor.matmul(psS[:, D:2 * D], ones[0:NP, :], root[0:NP, t, :], start=(t == 0), stop=(t == NT - 1))
                    ins.then_inc(bn_sq, 1)

        @block.vector
        def _(dve):
            v = nc.vector
            chain = [0]

            def link(ins):
                chain[0] += 1
                ins.then_inc(dve_chain, 1)
                dve.wait_ge(dve_chain, chain[0])

            def over_heads(a, n):
                return a.unsqueeze(len(a.shape)).broadcast_to(list(a.shape) + [n])

            def over_feats(a):
                return a.unsqueeze(2).broadcast_to([P, NT, D])

            def over_tiles(a):
                return a.unsqueeze(1).broadcast_to([P, NT, D])

            v.memset(dst_i[:], N).then_inc(cleared, 1)
            v.memset(src_i[:], 0).then_inc(cleared, 1)
            v.memset(xt[:], 0.0).then_inc(cleared, 1)
            v.memset(side[:], 0.0).then_inc(cleared, 1)
            v.memset(zeros_b[:], 0.0).then_inc(cleared, 1)
            v.memset(eps[:, 0:1], LN_EPS)
            v.memset(eps[:, 1:2], STD_EPS)
            link(v.memset(ones[:], 1.0))

            dve.wait_ge(dst_in, 32)
            link(v.memset(keep[:, 0, 0:1], 0.0))
            link(v.tensor_tensor(keep[:, 0, 1:LANE], dst_i[:, 1:LANE], dst_i[:, 0:LANE - 1], ALU.is_equal))
            link(v.tensor_scalar(keep[:, 1, :], keep[:, 0, :], -0.5, 2 * BIG, ALU.add, ALU.mult))
            link(v.tensor_scalar(fresh[:], keep[:, 0, :], -1.0, 1.0, ALU.mult, ALU.add))
            link(v.tensor_single_scalar(part_i, dst_i[:], P - 1, op=ALU.bitwise_and))
            link(v.tensor_copy(lo_hi[:, 0, :], part_i))
            link(v.tensor_single_scalar(part_i, dst_i[:], 7, op=ALU.arith_shift_right))
            link(v.tensor_copy(lo_hi[:, 1, :], part_i))
            v.tensor_copy(dfirst_i[:], dst_i[:, 0:1]).then_inc(lanes_rdy, 1)
            dve.wait_ge(lanes_rdy, 1)
            v.tensor_copy(dlast[:, 0, :], dst_i[:, LANE - 1:LANE].broadcast_to([P, P])).then_inc(dl_rdy, 1)
            for b in range(4):
                dve.wait_ge(wT_ps, b + 1)
                v.tensor_copy(wT[:, 4 * b:4 * b + 4, :], psT[b % 2][:].rearrange("p (k d) -> p k d", d=D)).then_inc(wT_rdy, 1)
            dve.wait_ge(dl_ps, 1)
            link(v.tensor_copy(dlast[:, 1, :], psL[:, 0:P]))
            link(v.memset(same[:, 0, 0:1], 0.0))
            link(v.tensor_tensor(same[:, 0, 1:P], dlast[:, 1, 1:P], dlast[:, 1, 0:P - 1], ALU.is_equal))
            link(v.tensor_scalar(same[:, 1, :], same[:, 0, :], -0.5, 2 * BIG, ALU.add, ALU.mult))
            dve.wait_ge(w_in, 16 * len(loads))
            link(v.tensor_tensor(att_sb[:, 0, :, :], att_sb[:, 0, :, :], w_att[:, :, 0:D], ALU.mult))
            link(v.tensor_tensor(att_sb[:, 1, :, :], att_sb[:, 1, :, :], w_d, ALU.mult))
            for k in range(2):
                for n in range(3):
                    link(v.reduce_sum(w_att[:, n, D + H * k:D + H * (k + 1)],
                                      att_sb[:, k, n, :].rearrange("p (h c) -> p h c", h=H), mybir.AxisListType.X))
            dve.wait_ge(x_in, 16)

            norm = 0
            for p in passes:
                g = p.number - GAT_FIRST
                if p.number in NORMED:
                    norm += 1
                    for t in range(NT):
                        ins = v.bn_stats(stats[:, t, :], xt[:, t, :])
                    link(ins)
                    for t in range(NT):
                        ins = v.bn_aggr(mv[:, t, :], stats[:, t, :])
                    ins.then_inc(var_rdy, 1)
                    dve.wait_ge(std_rdy, norm)
                    link(v.reciprocal(rstd[:], rstd[:]))
                    for t in range(NT):
                        ins = v.tensor_scalar(u[:, t, :], xt[:, t, :], mv[:, t, 0:1], rstd[:, t:t + 1],
                                              ALU.subtract, ALU.mult)
                    ins.then_inc(u_rdy, 1)
                y = ytab(p)
                if p.kind == GAT:
                    link(v.memset(y[:, :, C:GATW:HC], 1.0))
                for t in range(NT):
                    dve.wait_ge(y_ps, NT * p.number + t + 1)
                    pt = psY[t % 2]
                    if p.kind == GAT:
                        v.tensor_copy(y[:, t, 0:GATW].rearrange("p (h c) -> p h c", h=H)[:, :, 0:C],
                                      pt[:, 0:D].rearrange("p (h c) -> p h c", h=H)).then_inc(y_rdy, 1)
                        v.tensor_copy(y[:, t, GATW:GATW + 2 * H], pt[:, D:D + 2 * H]).then_inc(y_rdy, 1)
                    elif p.kind == MEAN0:
                        v.tensor_copy(y[:, t, :], pt[:, 0:D]).then_inc(y_rdy, 1)
                        v.tensor_copy(root[:, t, :], pt[:, 0:D]).then_inc(y_rdy, 1)
                    else:
                        bias = {PNA: BM, MEAN1: B1, MEAN2: B2}[p.kind]
                        v.tensor_copy(y[:, t, :], pt[:, 0:D]).then_inc(y_rdy, 1)
                        v.tensor_tensor(root[:, t, :], pt[:, D:2 * D], rowb[:, bias, :], ALU.add).then_inc(y_rdy, 1)
                if p.kind == GAT:
                    dve.wait_ge(ad_in, 16 * (g + 1))
                    link(v.tensor_tensor(ad_lane, ad_lane, over_heads(fresh[:], H), ALU.mult))
                    dve.wait_ge(ad_first_in, 16 * (g + 1))
                    link(v.tensor_copy(ad_lane[:, 0, :], ad_first[:, GATW + H:GATW + 2 * H]))
                    for h in range(H):
                        ins = v.tensor_tensor_scan(ad_lane[:, :, h], keep[:, 0, :], ad_lane[:, :, h], 0.0, ALU.mult, ALU.add)
                        link(ins)
                    link(v.memset(m_b[:, 0, :], 0.0))
                if p.number:
                    for r in range(ROWS_SLOTS):
                        dve.wait_ge(rows_out[r], p.rows0)
                dve.wait_ge(table_out, 16 * (p.number + 1))
                v.memset(state_rows(p, 1)[:, p.steps - 1, :], 0.0).then_inc(updated, 1)

                def group(rnd, s):
                    rows, r = gathered_rows(p, s), s % ROWS_SLOTS
                    state = state_rows(p, r)
                    prev = [state_rows(p, 1 - r)[:, p.steps - 1, :]] + [state[:, k, :] for k in range(p.steps - 1)]
                    n0 = p.steps0 + s * p.steps * p.ops
                    at = rnd * (SLOTS * p.steps * p.ops)
                    if p.number == 0:
                        if type(rnd) is not int or rnd > 0 or s >= 2:
                            dve.wait_ge(counted, rnd * SLOTS + (s - 1))
                        for c, (a, n) in enumerate(((0, P), (P, HI))):
                            digit = lo_hi[:, c, bass.ds(rnd * (SLOTS * p.steps) + s * p.steps, p.steps)]
                            v.tensor_tensor(onehot[:, s % 2, :, a:a + n],
                                            iota_lo[:, 0:n].unsqueeze(1).broadcast_to([P, p.steps, n]),
                                            digit.unsqueeze(2).broadcast_to([P, p.steps, n]),
                                            ALU.is_equal).then_inc(onehot_rdy, 1)
                    dve.wait_ge(gathered[s], p.gathered(rnd))
                    dve.wait_ge(keep_rdy, rnd * SLOTS + (p.groups0 + s + 1))
                    kw = keep_win[:, s, :, :]
                    if p.kind == GAT:
                        s0 = p.small0 + 12 * s
                        sat = rnd * (12 * SLOTS)

                        def after(n):
                            dve.wait_ge(small, sat + (s0 + n))

                        edges = bass.ds(rnd * (SLOTS * p.steps) + s * p.steps, p.steps)
                        v.tensor_tensor(e_b[:], rows[:, :, GATW:GATW + H], ad_lane[:, edges, :], ALU.add).then_inc(small, 1)
                        after(1)
                        v.scalar_tensor_tensor(e_b[:], e_b[:], NEG_SLOPE, e_b[:], ALU.mult, ALU.max).then_inc(small, 1)
                        after(2)
                        for h in range(H):
                            v.tensor_tensor_scan(m_b[:, 1:15, h], kw[:, 1, :], e_b[:, :, h], m_b[:, 0, h:h + 1],
                                                 ALU.min, ALU.max).then_inc(small, 1)
                        after(6)
                        v.tensor_tensor(d_b[:, 0, :, :], m_b[:, 0:14, :], over_heads(kw[:, 1, :], H), ALU.min).then_inc(small, 1)
                        after(7)
                        v.tensor_tensor(d_b[:, 0, :, :], d_b[:, 0, :, :], m_b[:, 1:15, :], ALU.subtract).then_inc(small, 1)
                        v.tensor_tensor(d_b[:, 1, :, :], e_b[:], m_b[:, 1:15, :], ALU.subtract).then_inc(small, 1)
                    if type(rnd) is not int or rnd > 0 or s >= ROWS_SLOTS:
                        dve.wait_ge(rows_out[r], rnd * (SLOTS // ROWS_SLOTS * 16) + (p.rows0 + s // ROWS_SLOTS * 16))
                    if p.kind == GAT:
                        v.tensor_copy(state[:, :, GATW:GATW + H], m_b[:, 1:15, :]).then_inc(small, 1)
                        v.tensor_copy(m_b[:, 0, :], m_b[:, 14, :]).then_inc(small, 1)
                        dve.wait_ge(exp_rdy, rnd * SLOTS + (p.exps0 + s + 1))
                        for_heads = rows[:, :, 0:GATW].rearrange("p k (h c) -> p k h c", h=H)
                        v.tensor_tensor(for_heads, for_heads, over_heads(cw_b[:, 1, :, :], HC), ALU.mult).then_inc(small, 1)
                        after(12)
                        for k in range(p.steps):
                            dve.wait_ge(updated, at + (n0 + 2 * k))
                            v.tensor_tensor(state[:, k, 0:GATW].rearrange("p (h c) -> p h c", h=H),
                                            prev[k][:, 0:GATW].rearrange("p (h c) -> p h c", h=H),
                                            over_heads(cw_b[:, 0, k, :], HC), ALU.mult).then_inc(updated, 1)
                            dve.wait_ge(updated, at + (n0 + 2 * k + 1))
                            v.tensor_tensor(state[:, k, 0:GATW], state[:, k, 0:GATW], rows[:, k, 0:GATW],
                                            ALU.add).then_inc(updated, 1)
                    elif p.kind == PNA:
                        dve.wait_ge(sq_rdy, rnd * (2 * SLOTS) + 2 * (s + 1))
                        for k in range(p.steps):
                            dve.wait_ge(updated, at + (n0 + 2 * k - (1 if s or k or type(rnd) is not int or rnd else 0)))
                            v.scalar_tensor_tensor(state[:, k, 0:2 * D], prev[k][:, 0:2 * D], kw[:, 0, k:k + 1],
                                                   rows[:, k, 0:2 * D], ALU.mult, ALU.add).then_inc(updated, 1)
                            dve.wait_ge(updated, at + (n0 + 2 * k))
                            v.scalar_tensor_tensor(state[:, k, 2 * D:4 * D], prev[k][:, 2 * D:4 * D], kw[:, 1, k:k + 1],
                                                   rows[:, k, D:3 * D], ALU.min, ALU.max).then_inc(updated, 1)
                    else:
                        for k in range(p.steps):
                            dve.wait_ge(updated, at + (n0 + k))
                            v.scalar_tensor_tensor(state[:, k, :], prev[k], kw[:, 0, k:k + 1], rows[:, k, :],
                                                   ALU.mult, ALU.add).then_inc(updated, 1)

                for s in range(SLOTS):
                    group(0, s)
                with dve.Fori(1, p.rounds, 1) as rnd:
                    for s in range(SLOTS):
                        group(rnd, s)
                dve.wait_ge(updated, p.updated(p.rounds - 1, SLOTS - 1))

                if p.number == 0:
                    dve.wait_ge(counted, p.groups + 1)
                    v.tensor_copy(hist[:], psH[0:HI, 0:P]).then_inc(hist_rdy, 1)
                    dve.wait_ge(deg_in, 16)
                    v.tensor_copy(tmp[:, 3, :], deg[:]).then_inc(ln_in, 1)
                    v.tensor_tensor_scan(tmp[:, 0, :], ones[:, 0:NT], deg[:], 0.0, ALU.mult, ALU.add).then_inc(sums_rdy, 1)
                    dve.wait_ge(sums_rdy, 1)
                    dve.wait_ge(base_ps, 1)
                    link(v.tensor_scalar(last[:], tmp[:, 0, :], psS[:, 0:1], None, ALU.add))
                    v.tensor_tensor(start[:], last[:], deg[:], ALU.subtract).then_inc(seg_rdy, 1)
                    dve.wait_ge(seg_rdy, 1)
                    v.tensor_scalar(last[:], last[:], -1.0, None, ALU.add).then_inc(seg_rdy, 1)
                    dve.wait_ge(seg_rdy, 2)
                    link(v.tensor_scalar(tmp[:, 1, :], last[:], 0.0, None, ALU.max))
                    v.tensor_copy(end_i[:], tmp[:, 1, :]).then_inc(index_rdy, 1)
                    link(v.tensor_scalar(has[:], deg[:], 0.0, None, ALU.is_gt))
                    link(v.tensor_scalar(nohas[:], has[:], -1.0, 1.0, ALU.mult, ALU.add))
                    link(v.tensor_scalar(tmp[:, 1, :], node_id[:], float(EP), None, ALU.add))
                    link(v.tensor_tensor(tmp[:, 1, :], tmp[:, 1, :], nohas[:], ALU.mult))
                    link(v.tensor_tensor(tmp[:, 2, :], start[:], has[:], ALU.mult))
                    link(v.tensor_tensor(tmp[:, 1, :], tmp[:, 1, :], tmp[:, 2, :], ALU.add))
                    v.tensor_copy(start_i[:], tmp[:, 1, :]).then_inc(index_rdy, 1)
                    link(v.tensor_scalar(tmp[:, 2, :], deg[:], 1.0, None, ALU.max))
                    link(v.reciprocal(tmp[:, 2, :], tmp[:, 2, :]))
                    link(v.tensor_tensor(hrec[:], tmp[:, 2, :], has[:], ALU.mult))
                    dve.wait_ge(ln_rdy, 1)
                    link(v.tensor_scalar(att[:], amp[:], 1e-30, None, ALU.add))
                    link(v.reciprocal(att[:], att[:]))
                    link(v.tensor_scalar(att[:], att[:], PNA_DELTA, None, ALU.mult))
                    link(v.tensor_scalar(amp[:], amp[:], 1.0 / PNA_DELTA, None, ALU.mult))
                    dve.wait_ge(seg_in, 32)
                    link(v.tensor_scalar(pick[:], bc_start, lane_last[:, 0:1], None, ALU.is_le))
                    link(v.scalar_tensor_tensor(pick[:], bc_last, lane_last[:, 0:1], pick[:], ALU.is_gt, ALU.mult))
                    v.scalar_tensor_tensor(pick[:], bc_last, lane_last[:, 1:2], pick[:], ALU.is_le, ALU.mult).then_inc(pick_rdy, 1)
                    dve.wait_ge(cross_ps, 1)
                    link(v.tensor_scalar(cbias[:], psS[:, 32:32 + NT], -1.0, BIG, ALU.add, ALU.mult))

                if p.kind == GAT:
                    lastrow = state_rows(p, 1)[:, p.steps - 1, :]
                    sums = lastrow[:, 0:GATW].rearrange("p (h c) -> p h c", h=H)
                    for k, a in enumerate((sums[:, :, 0:C], sums[:, :, C:HC].broadcast_to([P, H, C]),
                                           over_heads(lastrow[:, GATW:GATW + H], C))):
                        v.tensor_copy(lane_x[:, k, :].rearrange("p (h c) -> p h c", h=H), a).then_inc(laneL_rdy, 1)
                    dve.wait_ge(laneT_ps, p.number + 1)
                    num, den, mx = (psL[:, k * P:(k + 1) * P] for k in range(3))
                    link(v.tensor_tensor_scan(lane_s[:, 2, :], same[:, 1, :], mx, 0.0, ALU.min, ALU.max))
                    link(v.memset(lane_e[:, 0, 0:1], -BIG))
                    link(v.tensor_tensor(lane_e[:, 0, 1:P], lane_s[:, 2, 0:P - 1], same[:, 1, 1:P], ALU.min))
                    link(v.tensor_tensor(lane_e[:, 0, :], lane_e[:, 0, :], lane_s[:, 2, :], ALU.subtract))
                    v.tensor_tensor(lane_e[:, 1, :], mx, lane_s[:, 2, :], ALU.subtract).then_inc(laneE_in, 1)
                    dve.wait_ge(laneE_rdy, g + 1)
                    link(v.tensor_tensor(lane_x[:, 0, :], num, lane_e[:, 1, :], ALU.mult))
                    link(v.tensor_tensor(lane_x[:, 1, :], den, lane_e[:, 1, :], ALU.mult))
                    link(v.tensor_tensor_scan(lane_s[:, 0, :], lane_e[:, 0, :], lane_x[:, 0, :], 0.0, ALU.mult, ALU.add))
                    v.tensor_tensor_scan(lane_s[:, 1, :], lane_e[:, 0, :], lane_x[:, 1, :], 0.0, ALU.mult, ALU.add).then_inc(laneS_rdy, 1)
                    dve.wait_ge(laneZ_ps, p.number + 1)
                    z = Z[:, 0:GATW].rearrange("p (h c) -> p h c", h=H)
                    heads = [psZ[:, k * P:(k + 1) * P].rearrange("p (h c) -> p h c", h=H) for k in range(3)]
                    link(v.tensor_copy(z[:, :, 0:C], heads[0]))
                    link(v.tensor_copy(z[:, :, C:HC], heads[1][:, :, 0:1]))
                    v.tensor_copy(Z[:, GATW:GATW + H], heads[2][:, :, 0]).then_inc(Z_rdy, 1)
                else:
                    dve.wait_ge(laneT_ps, p.number + 1)
                    parts = 4 if p.kind == PNA else 1
                    for k in range(parts):
                        f, o0, o1 = (same[:, 0, :], ALU.mult, ALU.add) if k < 2 else (same[:, 1, :], ALU.min, ALU.max)
                        ins = v.tensor_tensor_scan(lane_s[:, k, :], f, psL[:, k * P:(k + 1) * P], 0.0, o0, o1)
                    ins.then_inc(laneS_rdy, 1)
                    dve.wait_ge(laneZ_ps, p.number + 1)
                    v.tensor_copy(Z[:, 0:p.state_w], psZ[:, 0:p.state_w]).then_inc(Z_rdy, 1)

                en = ends(p)
                dve.wait_ge(ends_in, 16 * NT * (p.number + 1))
                for t in range(NT):
                    dve.wait_ge(node_ps, NT * p.number + t + 1)
                    pt = psY[t % 2]
                    if p.kind == GAT:
                        v.tensor_copy(crossed[:, t, :], pt[:, 0:p.state_w]).then_inc(node_rdy, 1)
                    elif p.kind == PNA:
                        v.tensor_tensor(en[:, t, 0:2 * D], pt[:, 0:2 * D], en[:, t, 0:2 * D], ALU.add)
                        v.scalar_tensor_tensor(en[:, t, 2 * D:4 * D], pt[:, 2 * D:4 * D], cbias[:, t:t + 1],
                                               en[:, t, 2 * D:4 * D], ALU.add, ALU.max).then_inc(node_rdy, 1)
                    else:
                        v.tensor_tensor(en[:, t, :], pt[:, 0:D], en[:, t, :], ALU.add).then_inc(node_rdy, 1)
                dve.wait_ge(node_rdy, NT * (p.number + 1))

                if p.kind in (MEAN0, MEAN1, MEAN2):
                    link(v.tensor_tensor(en, en, over_feats(hrec[:]), ALU.mult))
                if p.kind == MEAN0:
                    link(v.tensor_tensor(root[:], root[:], over_feats(nohas[:]), ALU.mult))
                    link(v.tensor_tensor(en, en, root[:], ALU.add))
                    link(v.tensor_tensor(en, en, over_tiles(rowb[:, B0, :]), ALU.add))
                    link(v.tensor_scalar(en, en, 0.0, None, ALU.max))
                    link(v.tensor_tensor(xt[:], xt[:], en, ALU.add))
                if p.kind == MEAN1:
                    v.tensor_tensor(u, en, root[:], ALU.add).then_inc(u_rdy, 1)
                if p.kind == MEAN2:
                    link(v.tensor_tensor(en, en, root[:], ALU.add))
                    v.tensor_tensor(xt[:], xt[:], en, ALU.add).then_inc(done, 1)
                if p.kind == GAT:
                    me, mc = en[:, :, GATW:GATW + H], crossed[:, :, GATW:GATW + H]
                    link(v.tensor_tensor(sm[:, 0, :, 0:H], mc, over_heads(cbias[:], H), ALU.add))
                    link(v.tensor_tensor(sm[:, 0, :, H:2 * H], sm[:, 0, :, 0:H], me, ALU.max))
                    link(v.tensor_tensor(sm[:, 1, :, 0:H], me, sm[:, 0, :, H:2 * H], ALU.subtract))
                    v.tensor_tensor(sm[:, 1, :, H:2 * H], sm[:, 0, :, 0:H], sm[:, 0, :, H:2 * H], ALU.subtract).then_inc(ga_in, 1)
                    dve.wait_ge(ga_rdy, g + 1)
                    es = en[:, :, 0:GATW].rearrange("p t (h c) -> p t h c", h=H)
                    cs = crossed[:, :, 0:GATW].rearrange("p t (h c) -> p t h c", h=H)
                    link(v.tensor_tensor(es, es, over_heads(sm[:, 1, :, 0:H], HC), ALU.mult))
                    link(v.tensor_tensor(cs, cs, over_heads(sm[:, 1, :, H:2 * H], HC), ALU.mult))
                    link(v.tensor_tensor(en[:, :, 0:GATW], en[:, :, 0:GATW], crossed[:, :, 0:GATW], ALU.add))
                    link(v.tensor_scalar(rden[:], es[:, :, :, C], GAT_EPS, None, ALU.add))
                    link(v.reciprocal(rden[:], rden[:]))
                    link(v.tensor_tensor(rden[:], rden[:], over_heads(has[:], H), ALU.mult))
                    uh = u.rearrange("p t (h c) -> p t h c", h=H)
                    link(v.tensor_tensor(uh, es[:, :, :, 0:C], over_heads(rden[:], C), ALU.mult))
                    ins = v.tensor_tensor(u, u, over_tiles(rowb[:, BG + g, :]), ALU.add)
                    if g < 2:
                        ins.then_inc(u_rdy, 1)
                    else:
                        link(ins)
                        link(v.tensor_tensor(xt[:], xt[:], u, ALU.add))
                if p.kind == PNA:
                    sq, sm_, mx, nm = (en[:, :, k * D:(k + 1) * D] for k in range(4))
                    link(v.tensor_tensor(sm_, sm_, over_feats(hrec[:]), ALU.mult))
                    link(v.tensor_tensor(sq, sq, over_feats(hrec[:]), ALU.mult))
                    link(v.tensor_tensor(hbn, sm_, sm_, ALU.mult))
                    link(v.tensor_tensor(sq, sq, hbn, ALU.subtract))
                    v.tensor_scalar(sq, sq, 0.0, None, ALU.max).then_inc(sd_in, 1)
                    link(v.tensor_tensor(root[:], root[:], over_feats(has[:]), ALU.mult))
                    link(v.tensor_tensor(sm_, sm_, root[:], ALU.add))
                    link(v.tensor_tensor(mx, mx, over_feats(has[:]), ALU.mult))
                    link(v.tensor_tensor(mx, mx, root[:], ALU.add))
                    link(v.tensor_tensor(nm, nm, over_feats(has[:]), ALU.mult))
                    link(v.tensor_tensor(nm, root[:], nm, ALU.subtract))
                    dve.wait_ge(sd_rdy, 1)
                    v.tensor_copy(tmp[:, 0, 0:1], tmp[:, 1, 0:1]).then_inc(agg_rdy, 1)
                    for t in range(NT):
                        dve.wait_ge(pna_ps, t + 1)
                        pt, o = psY[t % 2], hbn[:, t, :]
                        link(v.tensor_tensor(o, pt[:, 3 * D:4 * D], rowb[:, BU, :], ALU.add))
                        link(v.tensor_tensor(o, pt[:, 0:D], o, ALU.add))
                        link(v.scalar_tensor_tensor(o, pt[:, D:2 * D], amp[:, t:t + 1], o, ALU.mult, ALU.add))
                        v.scalar_tensor_tensor(o, pt[:, 2 * D:3 * D], att[:, t:t + 1], o, ALU.mult, ALU.add).then_inc(pna_rdy, 1)
                    dve.wait_ge(pna_rdy, NT)
                    v.tensor_scalar(hbn, hbn, float(N) ** -0.5, None, ALU.mult).then_inc(bn_in, 1)
                    dve.wait_ge(bn_in, 1)
                    dve.wait_ge(bn_ps, 1)
                    link(v.tensor_scalar(bn[:, 0, :], psS[:, 0:D], 1.0 / N, None, ALU.mult))
                    link(v.tensor_tensor(hbn, hbn, over_tiles(bn[:, 0, :]), ALU.subtract))
                    v.tensor_tensor(root[:], hbn, hbn, ALU.mult).then_inc(bn_sq_in, 1)
                    dve.wait_ge(bn_sq, 1)
                    v.tensor_scalar(bn[:, 1, :], psS[:, D:2 * D], 1.0 / N, None, ALU.mult).then_inc(bn_var, 1)
                    dve.wait_ge(bn_std, 1)
                    link(v.reciprocal(bn[:, 1, :], bn[:, 2, :]))
                    link(v.tensor_tensor(bn[:, 1, :], bn[:, 1, :], rowb[:, BGAM, :], ALU.mult))
                    link(v.tensor_tensor(hbn, hbn, over_tiles(bn[:, 1, :]), ALU.mult))
                    link(v.tensor_tensor(hbn, hbn, over_tiles(rowb[:, BBET, :]), ALU.add))
                    link(v.tensor_tensor(xt[:], xt[:], hbn, ALU.add))


_INS = ["x", "src", "dst", "L0_gnn_W", "L0_gnn_b", "L1_gnn_Ws", "L1_gnn_Wd", "L1_gnn_att_s", "L1_gnn_att_d", "L1_gnn_b",
        "L2_gnn_M_w", "L2_gnn_M_b", "L2_gnn_U_w", "L2_gnn_U_b", "L2_gnn_bn_gamma", "L2_gnn_bn_beta",
        "L3_gnn_W1_neigh", "L3_gnn_W1_root", "L3_gnn_b1", "L3_gnn_W2_neigh", "L3_gnn_W2_root", "L3_gnn_b2"]


def kernel(**inputs):
    import numpy as _np
    import concourse.bacc as _bacc
    from concourse import mybir as _mybir
    from concourse.bass_utils import run_bass_kernel_spmd as _run

    nc = _bacc.Bacc("TRN2", target_bir_lowering=False, num_devices=1)
    arrays, args = {}, []
    for name in _INS:
        a = _np.ascontiguousarray(inputs[name])
        arrays[f"in_{name}_dram"] = a
        args.append(nc.dram_tensor(f"in_{name}_dram", a.shape, _mybir.dt.from_np(a.dtype), kind="ExternalInput").ap())
    x = inputs["x"]
    args.append(nc.dram_tensor("out_0_dram", tuple(x.shape), _mybir.dt.float32, kind="ExternalOutput").ap())
    build(nc, *args)
    r = _run(nc, [arrays], core_ids=[0])
    return r.results[0]["out_0_dram"]
```

```python
from contextlib import ExitStack

import concourse.bass as bass
from concourse import mybir

ALU = mybir.AluOpType
ACT = mybir.ActivationFunctionType
F32 = mybir.dt.float32
BF16 = mybir.dt.bfloat16
F16 = mybir.dt.float16
I32 = mybir.dt.int32

P = 128
D = 128
H = 4
C = D // H
HC = C + 1
GATW = H * HC
BIG = 1.5e38
NEG_SLOPE, GAT_EPS = 0.2, 1e-16
LN_EPS, BN_EPS, STD_EPS, PNA_DELTA = 1e-5, 1e-5, 1e-30, 2.5

MEAN0, GAT, PNA, MEAN1, MEAN2 = "mean0", "gat", "pna", "mean1", "mean2"
KINDS = [MEAN0, GAT, GAT, GAT, PNA, MEAN1, MEAN2]
GAT_FIRST, PNA_PASS, OUT_PASS = 1, 4, 6
NORMED = [0, 1, 4, 5]
SLOTS = 4
BT = 5
GAT_SMALL = 19
ROWS_SLOTS = 2


class Pass:

    def __init__(self, number, kind, lane, before):
        self.number, self.kind = number, kind
        self.steps = 7 if kind == PNA else 14
        self.by_pe = {GAT: 1, PNA: 0}.get(kind, 2)
        self.hots = 5 if kind == GAT else 25
        self.by_dma = self.steps - self.by_pe
        self.groups = lane // self.steps
        self.rounds = self.groups // SLOTS
        self.table_w = H * HC + 2 * H if kind == GAT else D
        self.step_w = {PNA: 3 * D, GAT: self.table_w}.get(kind, D)
        self.gather_at = D if kind == PNA else 0
        self.state_w = {PNA: 4 * D, GAT: GATW + H}.get(kind, D)
        self.group_updates = {GAT: self.steps + 1, PNA: 2 * self.steps}.get(kind, self.steps)
        self.updates = self.groups * self.group_updates
        b = before
        self.gathers0 = b.gathers0 + b.rounds * b.by_dma * 16 if b else 0
        self.groups0 = b.groups0 + b.groups if b else 0
        self.steps0 = (b.steps0 + b.updates if b else 0) + 1
        self.rows0 = b.rows0 + b.groups // ROWS_SLOTS * 16 if b else 0
        self.pe_groups0 = b.pe_groups0 + (b.groups if b.by_pe else 0) if b else 0
        self.src_bc0 = b.src_bc0 + (b.groups // 2 * 16 if b.by_pe else 0) if b else 0
        self.hots0_gat = b.hots0_gat + (b.groups * b.hots if b.kind == GAT else 0) if b else 0
        self.hots0 = b.hots0 + (b.groups * b.hots if b.by_pe else 0) if b else 0
        self.splits0 = b.splits0 + (5 if b.by_pe else 0) if b else 0
        self.small0 = b.small0 + (GAT_SMALL * b.groups if b.kind == GAT else 0) if b else 0
        self.exps0 = b.exps0 + (b.groups if b.kind == GAT else 0) if b else 0

    def gathered(self, rnd):
        return self.gathers0 + self.by_dma * 16 + rnd * (self.by_dma * 16)

    def updated(self, rnd, s):
        n = self.group_updates
        return rnd * (SLOTS * n) + (self.steps0 + (s + 1) * n)


def build(nc, x, src, dst, W0, b0, Ws, Wd, att_s, att_d, gat_b, M_w, M_b, U_w, U_b, gamma, beta,
          W1n, W1r, b1, W2n, W2r, b2, out):
    N, E = x.shape[0], src.shape[0]
    NT = 25
    NP = N // NT
    NN = P * NT
    NB = NT // BT
    MID = N // 2
    LANE = 784
    EP = P * LANE
    LAST_LANE = E - (P - 1) * LANE
    HI = NN // P
    assert N == NP * NT and NP <= P and 0 < LAST_LANE <= LANE and LANE % (14 * SLOTS) == 0

    passes = []
    for n, kind in enumerate(KINDS):
        passes.append(Pass(n, kind, LANE, passes[-1] if passes else None))
    GMAX = max(SLOTS * p.steps * p.step_w for p in passes)
    RMAX = max(ROWS_SLOTS * p.steps * p.state_w for p in passes)
    TW = max(p.table_w for p in passes)

    with ExitStack() as ctx:
        def sb(name, shape, dt=F32):
            return ctx.enter_context(nc.sbuf_tensor(name, shape, dt))

        def ps(name, shape):
            return ctx.enter_context(nc.psum_tensor(name, shape, F32))

        def sem(name):
            return ctx.enter_context(nc.semaphore(name))

        table_d = {w: nc.dram_tensor(f"table{w}", (NN, w), F32).ap() for w in {p.table_w for p in passes}}
        rows_d = {w: nc.dram_tensor(f"rows{w}", (EP, w), F32).ap() for w in {p.state_w for p in passes}}
        start_ad_d = nc.dram_tensor("start_ad", (EP + NN, H), F32).ap()
        pe_src_d = nc.dram_tensor("pe_src_d", (2 * LANE // 14 * P,), F16).ap()
        degree_d = nc.dram_tensor("degree", (NN,), F32).ap()
        start_d = nc.dram_tensor("start", (NN,), F32).ap()
        last_d = nc.dram_tensor("last", (NN,), F32).ap()

        xt = sb("xt", [P, NT, D])
        hT = sb("hT", [P, NT, P])
        root = sb("root", [P, NT, D])
        ring = sb("ring", [P, GMAX + RMAX])
        side = sb("side", [P, max(LANE * H, NT * (GATW + H))])
        pick = sb("pick", [P, NN])
        src_i = sb("src_i", [P, LANE], I32)
        dst_i = sb("dst_i", [P, LANE], I32)
        keep_all = sb("keep", [P, 2, LANE + 1])
        keep = keep_all[:, :, 0:LANE]
        fresh = sb("fresh", [P, LANE], BF16)
        src_win = sb("src_win", [P, SLOTS, 14], I32)
        keep_win = sb("keep_win", [P, SLOTS, 2, 14])
        iota_lo = sb("iota_lo", [P, P])
        zeros_b = sb("zeros_b", [P, P], BF16)
        ident = sb("ident", [P, P])
        ones = sb("ones", [P, P])
        before = sb("before", [P, P])
        lane_last = sb("lane_last", [P, 2])
        node_id = sb("node_id", [P, NT])
        same = sb("same", [P, 2, P])
        dfirst_i = sb("dfirst_i", [P, 1], I32)
        hist = sb("hist", [HI, P])
        deg = sb("deg", [P, NT])
        tmp = sb("tmp", [P, 4, NT])
        start = sb("start_s", [P, NT])
        last = sb("last_s", [P, NT])
        has = sb("has", [P, NT])
        nohas = sb("nohas", [P, NT])
        hrec = sb("hrec", [P, NT])
        cbias = sb("cbias", [P, NT])
        amp = sb("amp", [P, NT])
        att = sb("att", [P, NT])
        end_i = sb("end_i", [P, NT], I32)
        start_i = sb("start_i", [P, NT], I32)
        stats = sb("stats", [P, NT, 6])
        mv = sb("mv", [P, NT, 2])
        rstd = sb("rstd", [P, NT])
        wT = sb("wT", [P, 16, D])
        w_att = sb("w_att", [P, 3, GATW + H])
        w_sage = sb("w_sage", [P, 2, 2 * D])
        rowb = sb("rowb", [P, 10, D])
        B0, BG, BM, BU, BGAM, BBET, B1, B2 = 0, 1, 4, 5, 6, 7, 8, 9
        eps = sb("eps", [P, 2])
        span8 = sb("span8", [P, LANE], BF16)
        e_b = sb("e_b", [P, 15, H])
        top_b = sb("top_b", [P, 14, H])
        far_b = sb("far_b", [P, 14, H])
        m_b = sb("m_b", [P, 15, H])
        d_b = sb("d_b", [P, 15, H])
        cw_b = sb("cw_b", [P, 15, H])
        ad_first = sb("ad_first", [P, TW])
        lane_x = sb("lane_x", [P, 4, P])
        lane_s = sb("lane_s", [P, 4, P])
        lane_e = sb("lane_e", [P, 2, P])
        Z = sb("Z", [P, 4 * D])
        sm = sb("sm", [P, 3, NT, 2 * H])
        rden = sb("rden", [P, NT, H])
        bn = sb("bn", [P, 3, D])
        table_s = sb("table_s", [P, NT, 3, TW], BF16)
        src_bc = sb("src_bc", [P, 2, 2 * P], F16)
        node_c = sb("node_c", [P, NT])

        psT = [ps(f"psT{i}", [P, 512]) for i in range(2)]
        psY = [ps(f"psY{i}", [P, 512]) for i in range(2)]
        psL = ps("psL", [P, 512])
        psZ = ps("psZ", [P, 512])
        psH = ps("psH", [P, 512])
        psS = ps("psS", [P, 512])

        assert ROWS_SLOTS * passes[0].steps * passes[0].state_w <= RMAX - 25 * D
        flat = ring[:, GMAX + RMAX - 25 * D:GMAX + RMAX]
        w_raw = flat[:, 0:16 * D].rearrange("p (k d) -> p k d", d=D)
        w_d = flat[:, 16 * D:19 * D].rearrange("p (l d) -> p l d", d=D)
        att_sb = flat[:, 19 * D:25 * D].rearrange("p (a l d) -> p a l d", l=3, d=D)
        part_i = pick[:, 2 * LANE:3 * LANE].bitcast(I32)

        lo_hi = pick[:, 0:2 * LANE].rearrange("p (a j) -> p a j", a=2)
        onehot = side[:].bitcast(BF16)[:, 0:2 * 14 * (P + HI)].rearrange("p (a k w) -> p a k w", a=2, k=14)

        dlast = lane_s[:, 0:2, :]
        pe_src = Z[0:2 * LANE // 14, 0:P // 2].bitcast(F16)

        is_src = hT[:].rearrange("f t n -> f (t n)").bitcast(BF16).rearrange("p (t e) -> p t e", t=NT)

        def gathered_rows(p, s):
            n = p.steps * p.step_w
            return ring[:, s * n:(s + 1) * n].rearrange("p (k w) -> p k w", w=p.step_w)

        def state_rows(p, r):
            n = p.steps * p.state_w
            return ring[:, GMAX + r * n:GMAX + (r + 1) * n].rearrange("p (k w) -> p k w", w=p.state_w)

        def ytab(p):
            return ring[:, 0:NT * p.table_w].rearrange("p (t w) -> p t w", w=p.table_w)

        u = ring[:, NT * TW:NT * (TW + D)].rearrange("p (t w) -> p t w", w=D)
        bc_start = ring[:, 3400:3400 + NN]
        bc_last = ring[:, 3400 + NN:3400 + 2 * NN]
        assert 3400 + 2 * NN <= GMAX

        aggT = ring[:, NT * 4 * D:NT * 4 * D + 8 * P].rearrange("p (a w) -> p a w", a=2)
        mean_sq = ring[:, NT * 4 * D + 8 * P:NT * 4 * D + 8 * P + BT * D].rearrange("p (t d) -> p t d", d=D)
        rest = ring[:, NT * (TW + D):NT * (2 * TW + D)].rearrange("p (t w) -> p t w", w=TW)
        assert NT * (2 * TW + D) <= GMAX and NT * 4 * D + 8 * P <= GMAX + RMAX

        spans = [keep_all[:, 1, 1:LANE + 1], dst_i[:].bitcast(BF16)[:, 0:LANE],
                 dst_i[:].bitcast(BF16)[:, LANE:2 * LANE], span8[:]]

        def ends(p):
            return ring[:, 0:NT * p.state_w].rearrange("p (t w) -> p t w", w=p.state_w)

        def pick_t(t):
            return pick[:].rearrange("q (p t) -> q t p", t=NT)[:, t, :]

        ad_lane = side[:, 0:LANE * H].rearrange("p (j h) -> p j h", h=H)
        crossed = side[:, 0:NT * (GATW + H)].rearrange("p (t w) -> p t w", w=GATW + H)
        hbn = side[:, 0:NT * D].rearrange("p (t w) -> p t w", w=D)

        cleared = sem("cleared")
        src_in, dst_in, x_in = sem("src_in"), sem("dst_in"), sem("x_in")
        w0_in, w_in = sem("w0_in"), sem("w_in")
        w0_ps, w0_rdy = sem("w0_ps"), sem("w0_rdy")
        zero_in = sem("zero_in")
        const_rdy = sem("const_rdy")
        const_step = sem("const_step")
        wT_ps, wT_rdy = sem("wT_ps"), sem("wT_rdy")
        dl_ps = sem("dl_ps")
        dve_chain = sem("dve_chain")
        dl_rdy = sem("dl_rdy")
        lanes_rdy = sem("lanes_rdy")
        var_rdy, std_rdy = sem("var_rdy"), sem("std_rdy")
        u_rdy = sem("u_rdy")
        hT_ps, hT_rdy = sem("hT_ps"), sem("hT_rdy")
        y_ps, y_rdy = sem("y_ps"), sem("y_rdy")
        table_out = sem("table_out")
        ad_scattered = sem("ad_scattered")
        ad_in, ad_first_in = sem("ad_in"), sem("ad_first_in")
        gathered = [sem(f"gathered{s}") for s in range(SLOTS)]
        gate = sem("gate")
        pe_src_ps, pe_src_rdy, pe_src_out = sem("pe_src_ps"), sem("pe_src_rdy"), sem("pe_src_out")
        pe_cols = sem("pe_cols")
        src_bc_in = [sem(f"src_bc_in{z}") for z in range(2)]
        is_src_rdy = sem("is_src_rdy")
        distant = sem("distant")
        own_ps, own_rdy = sem("own_ps"), sem("own_rdy")
        fetched, fetched_rdy = sem("fetched"), sem("fetched_rdy")
        hi_rdy, rest_rdy, mid_rdy, split_rdy = sem("hi_rdy"), sem("rest_rdy"), sem("mid_rdy"), sem("split_rdy")
        src_rdy, keep_rdy = sem("src_rdy"), sem("keep_rdy")
        updated = sem("updated")
        small = sem("small")
        exp_in, exp_rdy = sem("exp_in"), sem("exp_rdy")
        sq_rdy = sem("sq_rdy")
        rows_out = [sem(f"rows_out{r}") for r in range(ROWS_SLOTS)]
        onehot_rdy, counted = sem("onehot_rdy"), sem("counted")
        hist_rdy, hist_out, deg_in = sem("hist_rdy"), sem("hist_out"), sem("deg_in")
        sums_rdy, base_ps = sem("sums_rdy"), sem("base_ps")
        seg_rdy, seg_out, seg_in = sem("seg_rdy"), sem("seg_out"), sem("seg_in")
        index_rdy = sem("index_rdy")
        pick_rdy, cross_ps = sem("pick_rdy"), sem("cross_ps")
        laneL_rdy = sem("laneL_rdy")
        laneT_ps = sem("laneT_ps")
        laneE_in, laneE_rdy = sem("laneE_in"), sem("laneE_rdy")
        laneS_rdy = sem("laneS_rdy")
        laneZ_ps, Z_rdy = sem("laneZ_ps"), sem("Z_rdy")
        node_ps, node_rdy = sem("node_ps"), sem("node_rdy")
        ends_in = [sem(f"ends_in{b}") for b in range(NB)]
        ga_in, ga_rdy = sem("ga_in"), sem("ga_rdy")
        ln_in, ln_rdy = sem("ln_in"), sem("ln_rdy")
        sd_in, sd_rdy = sem("sd_in"), sem("sd_rdy")
        agg_rdy = sem("agg_rdy")
        aggT_ps, aggT_rdy = sem("aggT_ps"), sem("aggT_rdy")
        pna_ps, pna_rdy = sem("pna_ps"), sem("pna_rdy")
        bn_dev = sem("bn_dev")
        bn_ps, bn_sq_in, bn_sq = sem("bn_ps"), sem("bn_sq_in"), sem("bn_sq")
        bn_var, bn_std = sem("bn_var"), sem("bn_std")
        done, stored = sem("done"), sem("stored")

        loads = [(w_raw[:, 1, :], M_w[:, 0:D]), (w_raw[:, 2, :], M_w[:, D:2 * D]),
                 (w_raw[:, 3:16, :], U_w.rearrange("o (k d) -> o k d", d=D)),
                 (w_att[:, :, 0:D], Ws.rearrange("l k n -> k l n")),
                 (w_d, Wd.rearrange("l k n -> k l n")),
                 (att_sb[:, 0, :, :], att_s.rearrange("l h c -> l (h c)").partition_broadcast(P)),
                 (att_sb[:, 1, :, :], att_d.rearrange("l h c -> l (h c)").partition_broadcast(P)),
                 (w_sage[:, 0, 0:D], W1n), (w_sage[:, 0, D:2 * D], W1r),
                 (w_sage[:, 1, 0:D], W2n), (w_sage[:, 1, D:2 * D], W2r),
                 (rowb[:, BG:BG + 3, :], gat_b.partition_broadcast(P))]
        loads += [(rowb[:, n, :], v.partition_broadcast(P))
                  for n, v in ((B0, b0), (BM, M_b), (BU, U_b), (BGAM, gamma), (BBET, beta), (B1, b1), (B2, b2))]

        block = ctx.enter_context(nc.Block())

        @block.sync
        def _(sp):
            sp.wait_ge(cleared, 1)
            sp.dma_start(xt[0:NP, :, :], x.rearrange("(p t) d -> p t d", t=NT)).then_inc(x_in, 16)
            sp.dma_start(w_raw[:, 0, :], W0).then_inc(w0_in, 16)
            sp.wait_ge(cleared, 2)
            sp.dma_start(src_i[0:P - 1, :], src[0:(P - 1) * LANE].rearrange("(p j) -> p j", j=LANE)).then_inc(src_in, 16)
            sp.dma_start(src_i[P - 1:P, 0:LAST_LANE],
                         src[(P - 1) * LANE:E].rearrange("(a j) -> a j", a=1)).then_inc(src_in, 16)
            sp.wait_ge(cleared, 3)
            sp.dma_start(dst_i[0:P - 1, :], dst[0:(P - 1) * LANE].rearrange("(p j) -> p j", j=LANE)).then_inc(dst_in, 16)
            sp.dma_start(dst_i[P - 1:P, 0:LAST_LANE],
                         dst[(P - 1) * LANE:E].rearrange("(a j) -> a j", a=1)).then_inc(dst_in, 16)
            for to, frm in loads:
                sp.dma_start(to, frm).then_inc(w_in, 16)
            for p in passes:
                for b in range(NB):
                    sp.wait_ge(y_rdy, 2 * NT * p.number + 2 * BT * (b + 1))
                    sp.dma_start(table_d[p.table_w].rearrange("(p t) w -> p t w", t=NT)[:, BT * b:BT * (b + 1), :],
                                 ytab(p)[:, BT * b:BT * (b + 1), :]).then_inc(table_out, 16)
                if p.number == 0:
                    sp.wait_ge(cleared, 4)
                    sp.dma_start(start_ad_d[0:EP, :].rearrange("(p j) h -> p (j h)", p=P),
                                 side[:, 0:LANE * H]).then_inc(zero_in, 16)
                    sp.wait_ge(pe_src_rdy, 1)
                    sp.dma_start(pe_src_d.rearrange("(k p) -> k p", p=P), pe_src).then_inc(pe_src_out, 16)
                    sp.wait_ge(pe_src_out, 16)
                if p.kind == GAT:
                    sp.wait_ge(ad_scattered, 16 * NT * (p.number - GAT_FIRST + 1))
                    sp.dma_start(ad_lane, start_ad_d[0:EP, :].rearrange("(p j) h -> p j h", p=P)).then_inc(ad_in, 16)
                lanes = rows_d[p.state_w].rearrange("(p j) w -> p j w", j=LANE)

                def broadcast(rnd, s):
                    n = p.by_pe * P
                    sp.dma_start(src_bc[:, s % 2, 0:n], pe_src_d[bass.ds(
                        rnd * (SLOTS * 2 * P) + (s * 2 * P + 2 * P - n), n)].partition_broadcast(P)).then_inc(src_bc_in[s % 2], 16)

                if p.by_pe and p.number:
                    sp.wait_ge(is_src_rdy, p.hots0)
                if p.by_pe:
                    broadcast(0, 0)
                    broadcast(0, 1)

                def store(rnd, final=False):
                    for s in range(SLOTS):
                        if p.by_pe and not (final and s >= SLOTS - 2):
                            sp.wait_ge(is_src_rdy, rnd * (p.hots * SLOTS) + (p.hots0 + p.hots * (s + 1)))
                            broadcast(rnd, s + 2)
                        sp.wait_ge(updated, p.updated(rnd, s))
                        sp.dma_start(lanes[:, bass.ds(rnd * (SLOTS * p.steps) + s * p.steps, p.steps), :],
                                     state_rows(p, s % ROWS_SLOTS)).then_inc(rows_out[s % ROWS_SLOTS], 16)

                with sp.Fori(0, p.rounds - 1, 1) as rnd:
                    store(rnd)
                store(p.rounds - 1, final=True)
                if p.number == 0:
                    sp.wait_ge(hist_rdy, 1)
                    sp.dma_start(degree_d.rearrange("(a b) -> a b", b=P), hist[:]).then_inc(hist_out, 16)
                    sp.wait_ge(hist_out, 16)
                    sp.dma_start(deg[:], degree_d.rearrange("(p t) -> p t", t=NT)).then_inc(deg_in, 16)
                    sp.wait_ge(seg_rdy, 2)
                    sp.dma_start(start_d.rearrange("(p t) -> p t", t=NT), start[:]).then_inc(seg_out, 16)
                    sp.dma_start(last_d.rearrange("(p t) -> p t", t=NT), last[:]).then_inc(seg_out, 16)
                    sp.wait_ge(seg_out, 32)
                    sp.dma_start(bc_start, start_d.partition_broadcast(P)).then_inc(seg_in, 16)
                    sp.dma_start(bc_last, last_d.partition_broadcast(P)).then_inc(seg_in, 16)
            for b in range(NB):
                sp.wait_ge(done, b + 1)
                sp.dma_start(out.rearrange("(p t) d -> p t d", t=NT)[:, BT * b:BT * (b + 1), :],
                             xt[0:NP, BT * b:BT * (b + 1), :]).then_inc(stored, 16)
            sp.wait_ge(stored, 16 * NB)
            sp.wait_ge(zero_in, 16)
            sp.wait_ge(table_out, 16 * NB * len(passes))
            for r in range(ROWS_SLOTS):
                sp.wait_ge(rows_out[r], passes[-1].rows0 + passes[-1].groups // ROWS_SLOTS * 16)

        @block.gpsimd
        def _(pool):
            pool.memset(ident[:], 0.0).then_inc(const_step, 1)
            pool.memset(before[:], 0.0).then_inc(const_step, 1)
            pool.wait_ge(const_step, 2)
            pool.affine_select(out=ident[:], in_=ident[:], compare_op=ALU.not_equal, fill=1.0, base=0,
                               pattern=[[-1, P]], channel_multiplier=1).then_inc(const_rdy, 1)
            pool.affine_select(out=before[:], in_=before[:], compare_op=ALU.is_ge, fill=1.0, base=0,
                               pattern=[[-1, P]], channel_multiplier=1).then_inc(const_rdy, 1)
            pool.iota(iota_lo[:], [[1, P]], base=0, channel_multiplier=0,
                      allow_small_or_imprecise_dtypes=True).then_inc(const_rdy, 1)
            pool.iota(lane_last[:], [[LANE, 2]], base=LANE - 1, channel_multiplier=LANE,
                      allow_small_or_imprecise_dtypes=True).then_inc(const_rdy, 1)
            pool.iota(node_id[:], [[1, NT]], base=0, channel_multiplier=NT,
                      allow_small_or_imprecise_dtypes=True).then_inc(const_rdy, 1)

            for p in passes:
                g = p.number - GAT_FIRST
                if p.kind == GAT:
                    pool.wait_ge(zero_in, 16)
                    if g:
                        pool.wait_ge(ad_in, 16 * g)
                    for t in range(NT):
                        pool.wait_ge(y_rdy, 2 * NT * p.number + 2 * (t + 1))
                        pool.indirect_dma_start(out=start_ad_d, out_offset=bass.IndirectOffsetOnAxis(
                            ap=start_i[:, t:t + 1], axis=0), in_=ytab(p)[:, t, GATW + H:GATW + 2 * H],
                            in_offset=None).then_inc(ad_scattered, 16)
                pool.wait_ge(table_out, 16 * NB * (p.number + 1))
                table = table_d[p.table_w]
                if p.kind == GAT:
                    pool.indirect_dma_start(out=ad_first[:, 0:p.table_w], out_offset=None, in_=table,
                                            in_offset=bass.IndirectOffsetOnAxis(ap=dfirst_i[:, 0:1], axis=0)
                                            ).then_inc(ad_first_in, 16)
                    pool.wait_ge(ad_scattered, 16 * NT * (g + 1))

                if p.by_pe:
                    pool.wait_ge(split_rdy, p.splits0 + 5)

                def gather(rnd):
                    for s in range(SLOTS):
                        pool.wait_ge(src_rdy, rnd * SLOTS + (p.groups0 + s + 1))
                        if type(rnd) is not int:
                            pool.sem_inc(gate, 1)
                        if type(rnd) is not int or rnd > 0:
                            pool.wait_ge(updated, p.updated(rnd - 1, s))
                            if type(rnd) is not int:
                                pool.sem_inc(gate, 1)
                        rows = gathered_rows(p, s)
                        for k in range(p.by_dma):
                            pool.indirect_dma_start(
                                out=rows[:, k, p.gather_at:p.gather_at + p.table_w], out_offset=None, in_=table,
                                in_offset=bass.IndirectOffsetOnAxis(ap=src_win[:, s, k:k + 1], axis=0)
                            ).then_inc(gathered[s], 16)

                gather(0)
                with pool.Fori(1, p.rounds, 1) as rnd:
                    gather(rnd)

                pool.wait_ge(index_rdy, 2)
                for r in range(ROWS_SLOTS):
                    pool.wait_ge(rows_out[r], p.rows0 + p.groups // ROWS_SLOTS * 16)
                pool.wait_ge(laneT_ps, p.number + 1)
                for t in range(NT):
                    pool.indirect_dma_start(out=ends(p)[:, t, :], out_offset=None, in_=rows_d[p.state_w],
                                            in_offset=bass.IndirectOffsetOnAxis(ap=end_i[:, t:t + 1], axis=0)
                                            ).then_inc(ends_in[t // BT], 16)

        @block.scalar
        def _(act):
            norm = 0
            act.wait_ge(src_in, 32)
            for p in passes:
                if p.number in NORMED:
                    norm += 1

                def deviation(b):
                    if p.number in NORMED and b < NB:
                        at = slice(BT * b, BT * (b + 1))
                        act.wait_ge(var_rdy, NB * (norm - 1) + b + 1)
                        nc.scalar.activation(rstd[:, at], mv[:, at, 1], ACT.Sqrt, bias=eps[:, 0:1]).then_inc(std_rdy, 1)

                deviation(0)
                deviation(1)
                for b in range(7):
                    k = min(4, NT - 4 * b)
                    act.wait_ge(hT_ps, 7 * p.number + b + 1)
                    nc.scalar.activation(hT[:, 4 * b:4 * b + k, :],
                                         psT[b % 2][:, 0:k * P].rearrange("f (t n) -> f t n", n=P),
                                         ACT.Relu).then_inc(hT_rdy, 1)
                    deviation(b + 2)

                for b in range(6 if p.by_pe else 0):
                    w = p.table_w
                    if b < 5:
                        act.wait_ge(y_rdy, 2 * NT * p.number + 10 * (b + 1))
                        nc.scalar.copy(table_s[:, 5 * b:5 * b + 5, 0, 0:w], ytab(p)[:, 5 * b:5 * b + 5, :]).then_inc(hi_rdy, 1)
                    if b >= 1:
                        act.wait_ge(rest_rdy, p.splits0 + b)
                        nc.scalar.copy(table_s[:, 5 * b - 5:5 * b, 1, 0:w], rest[:, 5 * b - 5:5 * b, 0:w]).then_inc(mid_rdy, 1)

                def window(rnd, s):
                    at = bass.ds(rnd * (SLOTS * p.steps) + s * p.steps, p.steps)
                    z = s % SLOTS
                    nc.scalar.copy(src_win[:, z, 0:p.steps], src_i[:, at]).then_inc(src_rdy, 1)
                    nc.scalar.copy(keep_win[:, z, :, 0:p.steps], keep[:, :, at]).then_inc(keep_rdy, 1)

                def fetch(rnd, s, final=False):
                    if not p.by_pe or final and s == SLOTS:
                        return
                    act.wait_ge(fetched, rnd * SLOTS + (p.pe_groups0 + s + 1))
                    z = s % SLOTS
                    if type(rnd) is not int or rnd > 0 or s >= SLOTS:
                        act.wait_ge(updated, p.updated(rnd - 1, s))
                    rows = gathered_rows(p, z)
                    for k in range(p.by_pe):
                        ins = nc.scalar.copy(rows[:, p.by_dma + k, p.gather_at:p.gather_at + p.table_w],
                                             psY[k][:, 0:p.table_w])
                    ins.then_inc(fetched_rdy, 1)

                def one_hots(rnd, s):
                    act.wait_ge(src_bc_in[s % 2], rnd * 32 + (p.src_bc0 + s // 2 * 16 + 16))
                    n = p.by_pe * P
                    for b in range(NB + 1):
                        if b < NB:
                            for t in range(BT * b, BT * (b + 1)):
                                ins = nc.scalar.activation(is_src[:, t, P:P + n], src_bc[:, s % 2, 0:n], ACT.Square,
                                                           bias=node_c[:, t:t + 1], scale=-1.0)
                            ins.then_inc(distant, 1)
                        if b:
                            act.wait_ge(distant, rnd * (NB * SLOTS) + (p.hots0_gat + NB * s + b))
                            at = slice(BT * (b - 1), BT * b)
                            nc.scalar.activation(is_src[:, at, 0:n], is_src[:, at, P:P + n], ACT.Relu,
                                                 bias=1.0, scale=-1.0).then_inc(is_src_rdy, 1)

                def group(rnd, s, final):
                    if not (final and s >= SLOTS - 2):
                        if type(rnd) is not int or rnd > 0 or s >= 2:
                            act.wait_ge(gathered[(s - 2) % SLOTS], p.gathered(rnd if s >= 2 else rnd - 1))
                            act.wait_ge(updated, p.updated(rnd, s - 2))
                        window(rnd, s + 2)
                    if p.kind == GAT:
                        act.wait_ge(small, rnd * (GAT_SMALL * SLOTS) + (p.small0 + GAT_SMALL * s + 16))
                        nc.scalar.activation(cw_b[:], d_b[:], ACT.Exp).then_inc(exp_rdy, 1)
                        fetch(rnd, s + 1, final)
                        if not (final and s >= SLOTS - 2):
                            one_hots(rnd, s + 2)
                    elif p.kind == PNA:
                        rows = gathered_rows(p, s)
                        act.wait_ge(gathered[s], p.gathered(rnd))
                        nc.scalar.activation(rows[:, :, 0:D], rows[:, :, D:2 * D], ACT.Square).then_inc(sq_rdy, 1)
                        nc.scalar.mul(rows[:, :, 2 * D:3 * D], rows[:, :, D:2 * D], -1.0).then_inc(sq_rdy, 1)
                    else:
                        fetch(rnd, s + 1, final)

                if p.number:
                    act.wait_ge(updated, p.steps0 - 1)
                if p.number == 0:
                    for s in range(2):
                        nc.scalar.copy(src_win[:, s, 0:p.steps], src_i[:, s * p.steps:(s + 1) * p.steps]).then_inc(src_rdy, 1)
                    act.wait_ge(lanes_rdy, 1)
                    for s in range(2):
                        nc.scalar.copy(keep_win[:, s, :, 0:p.steps],
                                       keep[:, :, s * p.steps:(s + 1) * p.steps]).then_inc(keep_rdy, 1)
                else:
                    window(0, 0)
                    window(0, 1)
                if p.by_pe:
                    act.wait_ge(split_rdy, p.splits0 + 5)
                    act.wait_ge(table_out, 16 * NB * (p.number + 1))
                    if p.kind == GAT:
                        one_hots(0, 0)
                        act.wait_ge(ad_scattered, 16 * NT * (p.number - GAT_FIRST + 1))
                    fetch(0, 0)
                    if p.kind == GAT:
                        one_hots(0, 1)
                for s in range(SLOTS):
                    group(0, s, False)
                with act.Fori(1, p.rounds - 1, 1) as rnd:
                    for s in range(SLOTS):
                        group(rnd, s, False)
                for s in range(SLOTS):
                    group(p.rounds - 1, s, True)

                if p.number == 0:
                    act.wait_ge(ln_in, 1)
                    nc.scalar.activation(amp[:], deg[:], ACT.Ln, bias=1.0).then_inc(ln_rdy, 1)
                if p.kind == GAT:
                    g = p.number - GAT_FIRST
                    act.wait_ge(laneE_in, g + 1)
                    nc.scalar.activation(lane_e[:], lane_e[:], ACT.Exp).then_inc(laneE_rdy, 1)
                    for b in range(NB):
                        at = slice(BT * b, BT * (b + 1))
                        act.wait_ge(ga_in, NB * g + b + 1)
                        nc.scalar.activation(sm[:, 1, at, :], sm[:, 1, at, :], ACT.Exp).then_inc(ga_rdy, 1)
                if p.kind == PNA:
                    for t in range(NT):
                        if t % BT == 0:
                            at = slice(t, t + BT)
                            act.wait_ge(sd_in, t // BT + 1)
                            nc.scalar.activation(ends(p)[:, at, 0:D], ends(p)[:, at, 0:D], ACT.Sqrt,
                                                 bias=eps[:, 1:2]).then_inc(sd_rdy, 1)
                        act.wait_ge(aggT_ps, t + 1)
                        if t >= 2:
                            act.wait_ge(pna_ps, t - 1)
                        nc.scalar.copy(aggT[:, t % 2, :], psT[t % 2][:]).then_inc(aggT_rdy, 1)
                    for b in range(NB):
                        at = slice(BT * b, BT * (b + 1))
                        act.wait_ge(bn_dev, b + 1)
                        nc.scalar.activation(root[:, at, :], hbn[:, at, :], ACT.Square).then_inc(bn_sq_in, 1)
                    act.wait_ge(bn_var, 1)
                    nc.scalar.activation(bn[:, 2, :], bn[:, 1, :], ACT.Sqrt, bias=eps[:, 0:1]).then_inc(bn_std, 1)

        @block.tensor
        def _(pe):
            pe.wait_ge(const_rdy, 5)
            pe.wait_ge(w0_in, 16)
            nc.tensor.transpose(psZ[:, 0:P], w_raw[:, 0, :], ident[:]).then_inc(w0_ps, 1)
            pe.wait_ge(w0_rdy, 1)

            for p in passes:
                g = p.number - GAT_FIRST
                for b in range(7):
                    if b >= 2:
                        pe.wait_ge(hT_rdy, 7 * p.number + b - 1)
                    pe.wait_ge(u_rdy, NB * p.number + min(4 * b + 3, NT - 1) // BT + 1)
                    for t in range(4 * b, min(4 * b + 4, NT)):
                        ins = nc.tensor.transpose(psT[b % 2][:, (t % 4) * P:(t % 4 + 1) * P], u[:, t, :], ident[:])
                    ins.then_inc(hT_ps, 1)
                w = {MEAN0: wT[:, 0, :], GAT: w_att[:, g % 3, :], PNA: wT[:, 1:3, :].rearrange("p a d -> p (a d)"),
                     MEAN1: w_sage[:, 0, :], MEAN2: w_sage[:, 1, :]}[p.kind]
                for t in range(NT):
                    pe.wait_ge(hT_rdy, 7 * p.number + t // 4 + 1)
                    if t >= 2:
                        pe.wait_ge(y_rdy, 2 * NT * p.number + 2 * (t - 1))
                    nc.tensor.matmul(psY[t % 2][:, 0:w.shape[1]], hT[:, t, :], w, start=True, stop=True).then_inc(y_ps, 1)

                def fetch(rnd):
                    for s in range(SLOTS):
                        for k in range(p.by_pe):
                            if type(rnd) is not int or rnd > 0 or s > 0:
                                if k == 0:
                                    pe.wait_ge(fetched_rdy, rnd * SLOTS + (p.pe_groups0 + s))
                            for t in range(NT):
                                if k == 0:
                                    pe.wait_ge(is_src_rdy, rnd * (p.hots * SLOTS)
                                               + (p.hots0 + p.hots * s + t * p.hots // NT + 1))
                                for c in range(3):
                                    ins = nc.tensor.matmul(psY[k][:, 0:p.table_w], is_src[:, t, k * P:(k + 1) * P],
                                                           table_s[:, t, c, 0:p.table_w],
                                                           start=(t == 0 and c == 0), stop=(t == NT - 1 and c == 2))
                        ins.then_inc(fetched, 1)
                        if p.number == 0:
                            count(rnd, s)

                pe.wait_ge(y_rdy, 2 * NT * (p.number + 1))
                if p.number == 0:
                    pe.wait_ge(dl_rdy, 1)
                    nc.tensor.transpose(psL[:, 0:P], dlast[:, 0, :], ident[:]).then_inc(dl_ps, 1)
                    pe.wait_ge(pe_cols, 1)
                    nc.tensor.transpose(psS[0:2 * LANE // 14, 0:P], lane_x[:, 0, 0:2 * LANE // 14],
                                        ident[:]).then_inc(pe_src_ps, 1)
                    pe.wait_ge(w_in, 16 * len(loads))
                    for b in range(4):
                        if b >= 2:
                            pe.wait_ge(wT_rdy, b - 1)
                        for k in range(1 if b == 0 else 0, 4):
                            ins = nc.tensor.transpose(psT[b % 2][:, k * P:(k + 1) * P], w_raw[:, 4 * b + k, :], ident[:])
                        ins.then_inc(wT_ps, 1)
                    pe.wait_ge(wT_rdy, 4)
                if p.kind == PNA:
                    for t in range(NT):
                        if t >= 2:
                            pe.wait_ge(own_rdy, t - 1)
                        nc.tensor.matmul(psY[t % 2][:, 0:D], hT[:, t, :], wT[:, 3, :], start=True, stop=True).then_inc(own_ps, 1)
                    pe.wait_ge(own_rdy, NT)
                if p.by_pe:
                    pe.wait_ge(split_rdy, p.splits0 + 5)

                if p.number == 0:
                    pe.wait_ge(cleared, 5)
                    nc.tensor.matmul(psH[0:HI, 0:P], zeros_b[:, 0:HI], zeros_b[:], start=True, stop=False,
                                     skip_group_check=True)

                    def count(rnd, s):
                        pe.wait_ge(onehot_rdy, rnd * (2 * SLOTS) + 2 * (s + 1))
                        for k in range(p.steps):
                            ins = nc.tensor.matmul(psH[0:HI, 0:P], onehot[:, s % 2, k, P:P + HI],
                                                   onehot[:, s % 2, k, 0:P], start=False, stop=False,
                                                   skip_group_check=True)
                        ins.then_inc(counted, 1)

                if p.by_pe:
                    fetch(0)
                    with pe.Fori(1, p.rounds, 1) as rnd:
                        fetch(rnd)
                if p.number == 0:
                    nc.tensor.matmul(psH[0:HI, 0:P], zeros_b[:, 0:HI], zeros_b[:], start=False, stop=True,
                                     skip_group_check=True).then_inc(counted, 1)
                    pe.wait_ge(sums_rdy, 1)
                    nc.tensor.matmul(psS[:, 0:1], before[:], tmp[:, 0, NT - 1:NT], start=True, stop=True).then_inc(base_ps, 1)
                    pe.wait_ge(pick_rdy, 1)
                    for t in range(NT):
                        ins = nc.tensor.matmul(psS[:, 32 + t:33 + t], pick_t(t), ones[:, 0:1], start=True, stop=True)
                    ins.then_inc(cross_ps, 1)

                parts = {GAT: 3, PNA: 4}.get(p.kind, 1)
                if p.kind == GAT:
                    pe.wait_ge(laneL_rdy, 3 * (g + 1))
                else:
                    pe.wait_ge(updated, p.updated(p.rounds - 1, SLOTS - 1))
                for k in range(parts):
                    frm = lane_x[:, k, :] if p.kind == GAT else state_rows(p, 1)[:, p.steps - 1, k * D:(k + 1) * D]
                    ins = nc.tensor.transpose(psL[:, k * P:(k + 1) * P], frm, ident[:])
                ins.then_inc(laneT_ps, 1)
                pe.wait_ge(laneS_rdy, p.number + 1)
                for k in range(parts):
                    ins = nc.tensor.transpose(psZ[:, k * P:(k + 1) * P], lane_s[:, k, :], ident[:])
                ins.then_inc(laneZ_ps, 1)
                pe.wait_ge(Z_rdy, p.number + 1)
                for t in range(NT):
                    if t >= 2:
                        pe.wait_ge(node_rdy, NT * p.number + t - 1)
                    nc.tensor.matmul(psY[t % 2][:, 0:p.state_w], pick_t(t), Z[:, 0:p.state_w],
                                     start=True, stop=True).then_inc(node_ps, 1)

                if p.kind == PNA:
                    pe.wait_ge(node_rdy, NT * (p.number + 1))

                    def node_sum(t):
                        pe.wait_ge(pna_rdy, t + 1)
                        return nc.tensor.matmul(psS[:, 0:D], ones[0:NP, :], hbn[0:NP, t, :], start=(t == 0), stop=(t == NT - 1))

                    for t in range(NT + 1):
                        if t < NT:
                            pe.wait_ge(agg_rdy, t // BT + 1)
                            pe.wait_ge(sd_rdy, t // BT + 1)
                            if t >= 2:
                                pe.wait_ge(aggT_rdy, t - 1)
                            for k in range(4):
                                ins = nc.tensor.transpose(psT[t % 2][:, k * P:(k + 1) * P],
                                                          ends(p)[:, t, k * D:(k + 1) * D], ident[:])
                            ins.then_inc(aggT_ps, 1)
                        if t >= 1:
                            v = t - 1
                            if v >= 2:
                                pe.wait_ge(pna_rdy, v - 1)
                            pe.wait_ge(aggT_rdy, v + 1)
                            for k, c in enumerate((3, 0, 1, 2)):
                                ins = nc.tensor.matmul(psY[v % 2][:, 0:3 * D].rearrange("n (f d) -> n f d", d=D),
                                                       aggT[:, v % 2, k * P:(k + 1) * P], wT[:, 4 + c:16:4, :],
                                                       start=(k == 0), stop=(k == 3), skip_group_check=True)
                            ins.then_inc(pna_ps, 1)
                            if v >= 2:
                                node_sum(v - 2)
                    node_sum(NT - 2)
                    node_sum(NT - 1).then_inc(bn_ps, 1)
                    for t in range(NT):
                        pe.wait_ge(bn_sq_in, t // BT + 1)
                        ins = nc.tensor.matmul(psS[:, D:2 * D], ones[0:NP, :], root[0:NP, t, :], start=(t == 0), stop=(t == NT - 1))
                    ins.then_inc(bn_sq, 1)

        @block.vector
        def _(dve):
            v = nc.vector
            chain = [0]

            def link(ins):
                chain[0] += 1
                ins.then_inc(dve_chain, 1)
                dve.wait_ge(dve_chain, chain[0])

            def over_heads(a, n):
                return a.unsqueeze(len(a.shape)).broadcast_to(list(a.shape) + [n])

            def over_feats(a):
                return a.unsqueeze(2).broadcast_to([P, a.shape[1], D])

            def over_tiles(a, n):
                return a.unsqueeze(1).broadcast_to([P, n, D])

            def moments(b):
                for t in range(BT * b, BT * (b + 1)):
                    ins = v.bn_stats(stats[:, t, :], xt[:, t, :])
                link(ins)
                for t in range(BT * b, BT * (b + 1)):
                    ins = v.bn_aggr(mv[:, t, :], stats[:, t, :])
                ins.then_inc(var_rdy, 1)

            def normalize(norm, b):
                at = slice(BT * b, BT * (b + 1))
                dve.wait_ge(std_rdy, NB * norm + b + 1)
                link(v.reciprocal(rstd[:, at], rstd[:, at]))
                for t in range(BT * b, BT * (b + 1)):
                    ins = v.tensor_scalar(u[:, t, :], xt[:, t, :], mv[:, t, 0:1], rstd[:, t:t + 1],
                                          ALU.subtract, ALU.mult)
                ins.then_inc(u_rdy, 1)

            v.memset(xt[:], 0.0).then_inc(cleared, 1)
            v.memset(src_i[:], 0).then_inc(cleared, 1)
            v.memset(dst_i[:], N).then_inc(cleared, 1)
            v.memset(side[:], 0.0).then_inc(cleared, 1)
            v.memset(zeros_b[:], 0.0).then_inc(cleared, 1)
            v.memset(eps[:, 0:1], LN_EPS)
            v.memset(eps[:, 1:2], STD_EPS)
            link(v.memset(ones[:], 1.0))
            dve.wait_ge(w0_ps, 1)
            v.tensor_copy(wT[:, 0, :], psZ[:, 0:P]).then_inc(w0_rdy, 1)
            dve.wait_ge(x_in, 16)

            def lanes():
                dve.wait_ge(src_in, 32)
                dve.wait_ge(const_rdy, 5)
                link(v.tensor_scalar(node_c[:], node_id[:], -float(MID), None, ALU.add))
                v.tensor_scalar(lane_x[:, 0, 0:2 * LANE // 14].rearrange("p (g m) -> p g m", m=2),
                                src_i[:].rearrange("p (g n) -> p g n", n=14)[:, :, 12:14], -float(MID), None,
                                ALU.add).then_inc(pe_cols, 1)
                dve.wait_ge(dst_in, 32)
                v.tensor_copy(dlast[:, 0, :], dst_i[:, LANE - 1:LANE].broadcast_to([P, P])).then_inc(dl_rdy, 1)
                dve.wait_ge(pe_src_ps, 1)
                v.tensor_copy(pe_src, psS[0:2 * LANE // 14, 0:P]).then_inc(pe_src_rdy, 1)
                link(v.memset(keep[:, 0, 0:1], 0.0))
                link(v.tensor_tensor(keep[:, 0, 1:LANE], dst_i[:, 1:LANE], dst_i[:, 0:LANE - 1], ALU.is_equal))
                link(v.tensor_scalar(keep[:, 1, :], keep[:, 0, :], -0.5, 2 * BIG, ALU.add, ALU.mult))
                link(v.tensor_scalar(fresh[:], keep[:, 0, :], -1.0, 1.0, ALU.mult, ALU.add))
                link(v.tensor_single_scalar(part_i, dst_i[:], P - 1, op=ALU.bitwise_and))
                link(v.tensor_copy(lo_hi[:, 0, :], part_i))
                link(v.tensor_single_scalar(part_i, dst_i[:], 7, op=ALU.arith_shift_right))
                link(v.tensor_copy(lo_hi[:, 1, :], part_i))
                v.tensor_copy(dfirst_i[:], dst_i[:, 0:1]).then_inc(lanes_rdy, 1)
                dve.wait_ge(lanes_rdy, 1)
                dve.wait_ge(dl_ps, 1)
                link(v.tensor_copy(dlast[:, 1, :], psL[:, 0:P]))
                link(v.memset(same[:, 0, 0:1], 0.0))
                link(v.tensor_tensor(same[:, 0, 1:P], dlast[:, 1, 1:P], dlast[:, 1, 0:P - 1], ALU.is_equal))
                link(v.tensor_scalar(same[:, 1, :], same[:, 0, :], -0.5, 2 * BIG, ALU.add, ALU.mult))

            def weights():
                for b in range(4):
                    dve.wait_ge(wT_ps, b + 1)
                    k = 1 if b == 0 else 0
                    v.tensor_copy(wT[:, 4 * b + k:4 * b + 4, :],
                                  psT[b % 2][:, k * P:4 * P].rearrange("p (k d) -> p k d", d=D)).then_inc(wT_rdy, 1)
                dve.wait_ge(w_in, 16 * len(loads))
                link(v.tensor_tensor(att_sb[:, 0, :, :], att_sb[:, 0, :, :], w_att[:, :, 0:D], ALU.mult))
                link(v.tensor_tensor(att_sb[:, 1, :, :], att_sb[:, 1, :, :], w_d, ALU.mult))
                for k in range(2):
                    for n in range(3):
                        link(v.reduce_sum(w_att[:, n, D + H * k:D + H * (k + 1)],
                                          att_sb[:, k, n, :].rearrange("p (h c) -> p h c", h=H), mybir.AxisListType.X))
                dve.wait_ge(zero_in, 16)

            for p in passes:
                g = p.number - GAT_FIRST
                if p.number == 0:
                    for b in range(NB + 1):
                        if b < NB:
                            moments(b)
                        if b:
                            normalize(0, b - 1)
                y = ytab(p)
                if p.kind == GAT:
                    link(v.memset(y[:, :, C:GATW:HC], 1.0))
                w = p.table_w

                def split(b):
                    if p.by_pe and 1 <= b <= 5:
                        at = slice(5 * b - 5, 5 * b)
                        dve.wait_ge(hi_rdy, p.splits0 + b)
                        dve.wait_ge(y_rdy, 2 * NT * p.number + 10 * b)
                        v.tensor_tensor(rest[:, at, 0:w], y[:, at, :], table_s[:, at, 0, 0:w], ALU.subtract).then_inc(rest_rdy, 1)
                    if p.by_pe and b >= 2:
                        at = slice(5 * b - 10, 5 * b - 5)
                        dve.wait_ge(mid_rdy, p.splits0 + b - 1)
                        v.tensor_tensor(table_s[:, at, 2, 0:w], rest[:, at, 0:w], table_s[:, at, 1, 0:w],
                                        ALU.subtract).then_inc(split_rdy, 1)

                for t in range(NT):
                    dve.wait_ge(y_ps, NT * p.number + t + 1)
                    pt = psY[t % 2]
                    if p.kind == GAT:
                        v.tensor_copy(y[:, t, 0:GATW].rearrange("p (h c) -> p h c", h=H)[:, :, 0:C],
                                      pt[:, 0:D].rearrange("p (h c) -> p h c", h=H)).then_inc(y_rdy, 1)
                        v.tensor_copy(y[:, t, GATW:GATW + 2 * H], pt[:, D:D + 2 * H]).then_inc(y_rdy, 1)
                    elif p.kind == MEAN0:
                        v.tensor_copy(y[:, t, :], pt[:, 0:D]).then_inc(y_rdy, 1)
                        v.tensor_copy(root[:, t, :], pt[:, 0:D]).then_inc(y_rdy, 1)
                    else:
                        bias = {PNA: BM, MEAN1: B1, MEAN2: B2}[p.kind]
                        v.tensor_copy(y[:, t, :], pt[:, 0:D]).then_inc(y_rdy, 1)
                        v.tensor_tensor(root[:, t, :], pt[:, D:2 * D], rowb[:, bias, :], ALU.add).then_inc(y_rdy, 1)
                    if t % 5 == 4:
                        split(t // 5)
                split(5)
                split(6)
                if p.number == 0:
                    lanes()
                    weights()
                if p.kind == GAT:
                    dve.wait_ge(ad_in, 16 * (g + 1))
                    link(v.tensor_tensor(ad_lane, ad_lane, over_heads(fresh[:], H), ALU.mult))
                    dve.wait_ge(ad_first_in, 16 * (g + 1))
                    link(v.tensor_copy(ad_lane[:, 0, :], ad_first[:, GATW + H:GATW + 2 * H]))
                    for h in range(H):
                        ins = v.tensor_tensor_scan(ad_lane[:, :, h], keep[:, 0, :], ad_lane[:, :, h], 0.0, ALU.mult, ALU.add)
                        link(ins)
                    link(v.memset(m_b[:, 0, :], 0.0))
                if p.kind == GAT and g == 2:
                    link(v.tensor_tensor(xt[:], xt[:], over_tiles(rowb[:, BG + g, :], NT), ALU.add))
                if p.kind == PNA:
                    dve.wait_ge(y_rdy, 2 * NT * (p.number + 1))
                    link(v.tensor_tensor(root[:], root[:], over_feats(has[:]), ALU.mult))
                    link(v.tensor_tensor(xt[:], xt[:], over_tiles(rowb[:, BBET, :], NT), ALU.add))
                    for t in range(NT):
                        dve.wait_ge(own_ps, t + 1)
                        v.tensor_tensor(hbn[:, t, :], psY[t % 2][:, 0:D], rowb[:, BU, :], ALU.add).then_inc(own_rdy, 1)
                    dve.wait_ge(own_rdy, NT)
                if p.kind == MEAN2:
                    dve.wait_ge(y_rdy, 2 * NT * (p.number + 1))
                    link(v.tensor_tensor(xt[:], xt[:], root[:], ALU.add))
                if p.number:
                    for r in range(ROWS_SLOTS):
                        dve.wait_ge(rows_out[r], p.rows0)
                dve.wait_ge(table_out, 16 * NB * (p.number + 1))
                v.memset(state_rows(p, 1)[:, p.steps - 1, :], 0.0).then_inc(updated, 1)

                def one_hots(rnd, s):
                    n = p.by_pe * P
                    if type(rnd) is not int or rnd > 0 or s > 0:
                        dve.wait_ge(fetched, rnd * SLOTS + (p.pe_groups0 + s))
                    dve.wait_ge(src_bc_in[s % 2], rnd * 32 + (p.src_bc0 + s // 2 * 16 + 16))
                    for t in range(NT):
                        v.tensor_scalar(is_src[:, t, 0:n], src_bc[:, s % 2, 0:n], node_c[:, t:t + 1], None,
                                        ALU.is_equal).then_inc(is_src_rdy, 1)

                if p.by_pe and p.kind != GAT:
                    one_hots(0, 0)
                if p.number == 0:
                    link(v.memset(e_b[:, 14, :], -BIG))
                    link(v.memset(keep_all[:, 1, LANE:LANE + 1], -BIG))
                    for i in range(1, 4):
                        n = 2 ** (i - 1)
                        link(v.memset(spans[i][:, LANE - n:LANE], -BIG))
                        link(v.tensor_tensor(spans[i][:, 0:LANE - n], spans[i - 1][:, 0:LANE - n],
                                             spans[i - 1][:, n:LANE], ALU.min))

                def group(rnd, s, final=False):
                    rows, r = gathered_rows(p, s), s % ROWS_SLOTS
                    state = state_rows(p, r)
                    prev = [state_rows(p, 1 - r)[:, p.steps - 1, :]] + [state[:, k, :] for k in range(p.steps - 1)]
                    n0 = p.steps0 + s * p.group_updates
                    at = rnd * (SLOTS * p.group_updates)
                    if p.number == 0:
                        if type(rnd) is not int or rnd > 0 or s >= 2:
                            dve.wait_ge(counted, rnd * SLOTS + (s - 1))
                        for c, (a, n) in enumerate(((0, P), (P, HI))):
                            digit = lo_hi[:, c, bass.ds(rnd * (SLOTS * p.steps) + s * p.steps, p.steps)]
                            v.tensor_tensor(onehot[:, s % 2, :, a:a + n],
                                            iota_lo[:, 0:n].unsqueeze(1).broadcast_to([P, p.steps, n]),
                                            digit.unsqueeze(2).broadcast_to([P, p.steps, n]),
                                            ALU.is_equal).then_inc(onehot_rdy, 1)
                    if p.by_pe:
                        if p.kind != GAT and not (final and s == SLOTS - 1):
                            one_hots(rnd, s + 1)
                        dve.wait_ge(fetched_rdy, rnd * SLOTS + (p.pe_groups0 + s + 1))
                    dve.wait_ge(gathered[s], p.gathered(rnd))
                    dve.wait_ge(keep_rdy, rnd * SLOTS + (p.groups0 + s + 1))
                    kw = keep_win[:, s, :, :]
                    if p.kind == GAT:
                        s0 = p.small0 + GAT_SMALL * s
                        sat = rnd * (GAT_SMALL * SLOTS)

                        def after(n):
                            dve.wait_ge(small, sat + (s0 + n))

                        edges = bass.ds(rnd * (SLOTS * p.steps) + s * p.steps, p.steps)
                        e = e_b[:, 0:p.steps, :]
                        v.tensor_tensor(e, rows[:, :, GATW:GATW + H], ad_lane[:, edges, :], ALU.add).then_inc(small, 1)
                        after(1)
                        v.scalar_tensor_tensor(e, e, NEG_SLOPE, e, ALU.mult, ALU.max).then_inc(small, 1)
                        frm = e_b
                        for i in range(4):
                            far = 2 ** i
                            n = p.steps + 1 - far if i == 0 else p.steps - far
                            linked = spans[i][:, bass.ds(rnd * (SLOTS * p.steps) + s * p.steps, n)]
                            after(2 + 2 * i)
                            v.tensor_tensor(far_b[:, 0:n, :], frm[:, far:far + n, :], over_heads(linked, H),
                                            ALU.min).then_inc(small, 1)
                            after(3 + 2 * i)
                            v.tensor_tensor(top_b[:, 0:n, :], frm[:, 0:n, :], far_b[:, 0:n, :], ALU.max).then_inc(small, 1)
                            frm = top_b
                        after(10)
                        for h in range(H):
                            v.tensor_tensor_scan(m_b[:, 1:15, h], kw[:, 1, :], top_b[:, :, h], m_b[:, 0, h:h + 1],
                                                 ALU.min, ALU.max).then_inc(small, 1)
                        after(14)
                        v.scalar_tensor_tensor(d_b[:, 0, :], m_b[:, 0, :], kw[:, 1, 0:1], m_b[:, 1, :],
                                               ALU.min, ALU.subtract).then_inc(small, 1)
                        v.tensor_tensor(d_b[:, 1:15, :], e, m_b[:, 1:15, :], ALU.subtract).then_inc(small, 1)
                    if type(rnd) is not int or rnd > 0 or s >= ROWS_SLOTS:
                        dve.wait_ge(rows_out[r], rnd * (SLOTS // ROWS_SLOTS * 16) + (p.rows0 + s // ROWS_SLOTS * 16))
                    if p.kind == GAT:
                        v.tensor_copy(state[:, :, GATW:GATW + H], m_b[:, 1:15, :]).then_inc(small, 1)
                        after(15)
                        v.tensor_copy(m_b[:, 0, :], m_b[:, 14, :]).then_inc(small, 1)
                        dve.wait_ge(exp_rdy, rnd * SLOTS + (p.exps0 + s + 1))
                        for_heads = rows[:, :, 0:GATW].rearrange("p k (h c) -> p k h c", h=H)
                        v.tensor_tensor(for_heads, for_heads, over_heads(cw_b[:, 1:15, :], HC), ALU.mult).then_inc(small, 1)
                        after(GAT_SMALL)
                        dve.wait_ge(updated, at + n0)
                        v.tensor_tensor(state[:, 0, 0:GATW].rearrange("p (h c) -> p h c", h=H),
                                        prev[0][:, 0:GATW].rearrange("p (h c) -> p h c", h=H),
                                        over_heads(cw_b[:, 0, :], HC), ALU.mult).then_inc(updated, 1)
                        dve.wait_ge(updated, at + (n0 + 1))
                        v.tensor_tensor(state[:, 0, 0:GATW], state[:, 0, 0:GATW], rows[:, 0, 0:GATW],
                                        ALU.add).then_inc(updated, 1)
                        for k in range(1, p.steps):
                            dve.wait_ge(updated, at + (n0 + k + 1))
                            v.scalar_tensor_tensor(state[:, k, 0:GATW], prev[k][:, 0:GATW], kw[:, 0, k:k + 1],
                                                   rows[:, k, 0:GATW], ALU.mult, ALU.add).then_inc(updated, 1)
                    elif p.kind == PNA:
                        dve.wait_ge(sq_rdy, rnd * (2 * SLOTS) + 2 * (s + 1))
                        for k in range(p.steps):
                            dve.wait_ge(updated, at + (n0 + 2 * k - (1 if s or k or type(rnd) is not int or rnd else 0)))
                            v.scalar_tensor_tensor(state[:, k, 0:2 * D], prev[k][:, 0:2 * D], kw[:, 0, k:k + 1],
                                                   rows[:, k, 0:2 * D], ALU.mult, ALU.add).then_inc(updated, 1)
                            dve.wait_ge(updated, at + (n0 + 2 * k))
                            v.scalar_tensor_tensor(state[:, k, 2 * D:4 * D], prev[k][:, 2 * D:4 * D], kw[:, 1, k:k + 1],
                                                   rows[:, k, D:3 * D], ALU.min, ALU.max).then_inc(updated, 1)
                    else:
                        for k in range(p.steps):
                            dve.wait_ge(updated, at + (n0 + k))
                            v.scalar_tensor_tensor(state[:, k, :], prev[k], kw[:, 0, k:k + 1], rows[:, k, :],
                                                   ALU.mult, ALU.add).then_inc(updated, 1)

                for s in range(SLOTS):
                    group(0, s)
                with dve.Fori(1, p.rounds - 1, 1) as rnd:
                    for s in range(SLOTS):
                        group(rnd, s)
                for s in range(SLOTS):
                    group(p.rounds - 1, s, final=True)
                dve.wait_ge(updated, p.updated(p.rounds - 1, SLOTS - 1))

                if p.number == 0:
                    dve.wait_ge(counted, p.groups + 1)
                    v.tensor_copy(hist[:], psH[0:HI, 0:P]).then_inc(hist_rdy, 1)
                    dve.wait_ge(deg_in, 16)
                    v.tensor_copy(tmp[:, 3, :], deg[:]).then_inc(ln_in, 1)
                    v.tensor_tensor_scan(tmp[:, 0, :], ones[:, 0:NT], deg[:], 0.0, ALU.mult, ALU.add).then_inc(sums_rdy, 1)
                    dve.wait_ge(sums_rdy, 1)
                    dve.wait_ge(base_ps, 1)
                    link(v.tensor_scalar(last[:], tmp[:, 0, :], psS[:, 0:1], None, ALU.add))
                    v.tensor_tensor(start[:], last[:], deg[:], ALU.subtract).then_inc(seg_rdy, 1)
                    dve.wait_ge(seg_rdy, 1)
                    v.tensor_scalar(last[:], last[:], -1.0, None, ALU.add).then_inc(seg_rdy, 1)
                    dve.wait_ge(seg_rdy, 2)
                    link(v.tensor_scalar(tmp[:, 1, :], last[:], 0.0, None, ALU.max))
                    v.tensor_copy(end_i[:], tmp[:, 1, :]).then_inc(index_rdy, 1)
                    link(v.tensor_scalar(has[:], deg[:], 0.0, None, ALU.is_gt))
                    link(v.tensor_scalar(nohas[:], has[:], -1.0, 1.0, ALU.mult, ALU.add))
                    link(v.tensor_scalar(tmp[:, 1, :], node_id[:], float(EP), None, ALU.add))
                    link(v.tensor_tensor(tmp[:, 1, :], tmp[:, 1, :], nohas[:], ALU.mult))
                    link(v.tensor_tensor(tmp[:, 2, :], start[:], has[:], ALU.mult))
                    link(v.tensor_tensor(tmp[:, 1, :], tmp[:, 1, :], tmp[:, 2, :], ALU.add))
                    v.tensor_copy(start_i[:], tmp[:, 1, :]).then_inc(index_rdy, 1)
                    link(v.tensor_scalar(tmp[:, 2, :], deg[:], 1.0, None, ALU.max))
                    link(v.reciprocal(tmp[:, 2, :], tmp[:, 2, :]))
                    link(v.tensor_tensor(hrec[:], tmp[:, 2, :], has[:], ALU.mult))
                    dve.wait_ge(ln_rdy, 1)
                    link(v.tensor_tensor(amp[:], amp[:], has[:], ALU.mult))
                    link(v.tensor_scalar(att[:], amp[:], 1e-30, None, ALU.add))
                    link(v.reciprocal(att[:], att[:]))
                    link(v.tensor_scalar(att[:], att[:], PNA_DELTA, None, ALU.mult))
                    link(v.tensor_scalar(amp[:], amp[:], 1.0 / PNA_DELTA, None, ALU.mult))
                    dve.wait_ge(seg_in, 32)
                    link(v.tensor_scalar(pick[:], bc_start, lane_last[:, 0:1], None, ALU.is_le))
                    link(v.scalar_tensor_tensor(pick[:], bc_last, lane_last[:, 0:1], pick[:], ALU.is_gt, ALU.mult))
                    v.scalar_tensor_tensor(pick[:], bc_last, lane_last[:, 1:2], pick[:], ALU.is_le, ALU.mult).then_inc(pick_rdy, 1)
                    dve.wait_ge(cross_ps, 1)
                    link(v.tensor_scalar(cbias[:], psS[:, 32:32 + NT], -1.0, BIG, ALU.add, ALU.mult))

                if p.kind == GAT:
                    lastrow = state_rows(p, 1)[:, p.steps - 1, :]
                    sums = lastrow[:, 0:GATW].rearrange("p (h c) -> p h c", h=H)
                    for k, a in enumerate((sums[:, :, 0:C], sums[:, :, C:HC].broadcast_to([P, H, C]),
                                           over_heads(lastrow[:, GATW:GATW + H], C))):
                        v.tensor_copy(lane_x[:, k, :].rearrange("p (h c) -> p h c", h=H), a).then_inc(laneL_rdy, 1)
                    dve.wait_ge(laneT_ps, p.number + 1)
                    num, den, mx = (psL[:, k * P:(k + 1) * P] for k in range(3))
                    link(v.tensor_tensor_scan(lane_s[:, 2, :], same[:, 1, :], mx, 0.0, ALU.min, ALU.max))
                    link(v.memset(lane_e[:, 0, 0:1], -BIG))
                    link(v.tensor_tensor(lane_e[:, 0, 1:P], lane_s[:, 2, 0:P - 1], same[:, 1, 1:P], ALU.min))
                    link(v.tensor_tensor(lane_e[:, 0, :], lane_e[:, 0, :], lane_s[:, 2, :], ALU.subtract))
                    v.tensor_tensor(lane_e[:, 1, :], mx, lane_s[:, 2, :], ALU.subtract).then_inc(laneE_in, 1)
                    dve.wait_ge(laneE_rdy, g + 1)
                    link(v.tensor_tensor(lane_x[:, 0, :], num, lane_e[:, 1, :], ALU.mult))
                    link(v.tensor_tensor(lane_x[:, 1, :], den, lane_e[:, 1, :], ALU.mult))
                    link(v.tensor_tensor_scan(lane_s[:, 0, :], lane_e[:, 0, :], lane_x[:, 0, :], 0.0, ALU.mult, ALU.add))
                    v.tensor_tensor_scan(lane_s[:, 1, :], lane_e[:, 0, :], lane_x[:, 1, :], 0.0, ALU.mult, ALU.add).then_inc(laneS_rdy, 1)
                    dve.wait_ge(laneZ_ps, p.number + 1)
                    z = Z[:, 0:GATW].rearrange("p (h c) -> p h c", h=H)
                    heads = [psZ[:, k * P:(k + 1) * P].rearrange("p (h c) -> p h c", h=H) for k in range(3)]
                    link(v.tensor_copy(z[:, :, 0:C], heads[0]))
                    link(v.tensor_copy(z[:, :, C:HC], heads[1][:, :, 0:1]))
                    v.tensor_copy(Z[:, GATW:GATW + H], heads[2][:, :, 0]).then_inc(Z_rdy, 1)
                else:
                    dve.wait_ge(laneT_ps, p.number + 1)
                    parts = 4 if p.kind == PNA else 1
                    for k in range(parts):
                        f, o0, o1 = (same[:, 0, :], ALU.mult, ALU.add) if k < 2 else (same[:, 1, :], ALU.min, ALU.max)
                        ins = v.tensor_tensor_scan(lane_s[:, k, :], f, psL[:, k * P:(k + 1) * P], 0.0, o0, o1)
                    ins.then_inc(laneS_rdy, 1)
                    dve.wait_ge(laneZ_ps, p.number + 1)
                    v.tensor_copy(Z[:, 0:p.state_w], psZ[:, 0:p.state_w]).then_inc(Z_rdy, 1)

                en = ends(p)

                def node_states(b):
                    dve.wait_ge(ends_in[b], 16 * BT * (p.number + 1))
                    for t in range(BT * b, BT * (b + 1)):
                        dve.wait_ge(node_ps, NT * p.number + t + 1)
                        pt = psY[t % 2]
                        if p.kind == GAT:
                            v.tensor_copy(crossed[:, t, :], pt[:, 0:p.state_w]).then_inc(node_rdy, 1)
                        elif p.kind == PNA:
                            v.tensor_tensor(en[:, t, 0:2 * D], pt[:, 0:2 * D], en[:, t, 0:2 * D], ALU.add)
                            v.scalar_tensor_tensor(en[:, t, 2 * D:4 * D], pt[:, 2 * D:4 * D], cbias[:, t:t + 1],
                                                   en[:, t, 2 * D:4 * D], ALU.add, ALU.max).then_inc(node_rdy, 1)
                        else:
                            v.tensor_tensor(en[:, t, :], pt[:, 0:D], en[:, t, :], ALU.add).then_inc(node_rdy, 1)
                    dve.wait_ge(node_rdy, NT * p.number + BT * (b + 1))
                    if p.kind == GAT:
                        at = slice(BT * b, BT * (b + 1))
                        me, mc = en[:, at, GATW:GATW + H], crossed[:, at, GATW:GATW + H]
                        link(v.tensor_tensor(sm[:, 0, at, 0:H], mc, over_heads(cbias[:, at], H), ALU.add))
                        link(v.tensor_tensor(sm[:, 0, at, H:2 * H], sm[:, 0, at, 0:H], me, ALU.max))
                        link(v.tensor_tensor(sm[:, 1, at, 0:H], me, sm[:, 0, at, H:2 * H], ALU.subtract))
                        v.tensor_tensor(sm[:, 1, at, H:2 * H], sm[:, 0, at, 0:H], sm[:, 0, at, H:2 * H],
                                        ALU.subtract).then_inc(ga_in, 1)

                def layer_out(b):
                    at = slice(BT * b, BT * (b + 1))
                    e, x_, r_ = en[:, at, :], xt[:, at, :], root[:, at, :]
                    if p.kind in (MEAN0, MEAN1, MEAN2):
                        link(v.tensor_tensor(e, e, over_feats(hrec[:, at]), ALU.mult))
                    if p.kind == MEAN0:
                        link(v.tensor_tensor(e, e, r_, ALU.add))
                        link(v.scalar_tensor_tensor(x_, e, 0.0, x_, ALU.max, ALU.add))
                    if p.kind == MEAN1:
                        v.tensor_tensor(u[:, at, :], e, r_, ALU.add).then_inc(u_rdy, 1)
                    if p.kind == MEAN2:
                        v.tensor_tensor(x_, x_, e, ALU.add).then_inc(done, 1)
                    if p.kind == GAT:
                        dve.wait_ge(ga_rdy, NB * g + b + 1)
                        c_ = crossed[:, at, :]
                        es = e[:, :, 0:GATW].rearrange("p t (h c) -> p t h c", h=H)
                        cs = c_[:, :, 0:GATW].rearrange("p t (h c) -> p t h c", h=H)
                        v.tensor_tensor(es, es, over_heads(sm[:, 1, at, 0:H], HC), ALU.mult)
                        link(v.tensor_tensor(cs, cs, over_heads(sm[:, 1, at, H:2 * H], HC), ALU.mult))
                        link(v.tensor_tensor(e[:, :, 0:GATW], e[:, :, 0:GATW], c_[:, :, 0:GATW], ALU.add))
                        rd = rden[:, at, :]
                        link(v.tensor_scalar(rd, es[:, :, :, C], GAT_EPS, None, ALU.add))
                        link(v.reciprocal(rd, rd))
                        link(v.tensor_tensor(rd, rd, over_heads(has[:, at], H), ALU.mult))
                        ub = u[:, at, :]
                        link(v.tensor_tensor(ub.rearrange("p t (h c) -> p t h c", h=H), es[:, :, :, 0:C],
                                             over_heads(rd, C), ALU.mult))
                        if g < 2:
                            v.tensor_tensor(ub, ub, over_tiles(rowb[:, BG + g, :], BT), ALU.add).then_inc(u_rdy, 1)
                        else:
                            link(v.tensor_tensor(x_, x_, ub, ALU.add))
                    if p.kind == PNA:
                        sq, sm_, mx, nm = (e[:, :, k * D:(k + 1) * D] for k in range(4))
                        v.tensor_tensor(sq, sq, over_feats(hrec[:, at]), ALU.mult)
                        link(v.tensor_tensor(sm_, sm_, over_feats(hrec[:, at]), ALU.mult))
                        v.tensor_tensor(mx, mx, over_feats(has[:, at]), ALU.mult)
                        link(v.tensor_tensor(mean_sq, sm_, sm_, ALU.mult))
                        v.tensor_tensor(nm, nm, over_feats(has[:, at]), ALU.mult)
                        link(v.tensor_tensor(sq, sq, mean_sq, ALU.subtract))
                        v.tensor_scalar(sq, sq, 0.0, None, ALU.max).then_inc(sd_in, 1)
                        v.tensor_tensor(sm_, sm_, r_, ALU.add)
                        link(v.tensor_tensor(mx, mx, r_, ALU.add))
                        v.tensor_tensor(nm, r_, nm, ALU.subtract).then_inc(agg_rdy, 1)

                if p.kind == MEAN0:
                    link(v.tensor_tensor(root[:], root[:], over_feats(nohas[:]), ALU.mult))
                    link(v.tensor_tensor(root[:], root[:], over_tiles(rowb[:, B0, :], NT), ALU.add))
                next_normed = p.number + 1 in NORMED
                for b in range(NB + 2):
                    if b < NB:
                        node_states(b)
                    if 1 <= b <= NB:
                        layer_out(b - 1)
                        if next_normed and p.kind != PNA:
                            moments(b - 1)
                if p.kind == PNA:
                    for t in range(NT):
                        dve.wait_ge(pna_ps, t + 1)
                        pt, o = psY[t % 2], hbn[:, t, :]
                        link(v.tensor_tensor(o, pt[:, 0:D], o, ALU.add))
                        link(v.scalar_tensor_tensor(o, pt[:, D:2 * D], amp[:, t:t + 1], o, ALU.mult, ALU.add))
                        v.scalar_tensor_tensor(o, pt[:, 2 * D:3 * D], att[:, t:t + 1], o, ALU.mult, ALU.add).then_inc(pna_rdy, 1)
                    dve.wait_ge(bn_ps, 1)
                    link(v.tensor_scalar(bn[:, 0, :], psS[:, 0:D], 1.0 / N, None, ALU.mult))
                    for b in range(NB):
                        hb = hbn[:, BT * b:BT * (b + 1), :]
                        v.tensor_tensor(hb, hb, over_tiles(bn[:, 0, :], BT), ALU.subtract).then_inc(bn_dev, 1)
                    dve.wait_ge(bn_dev, NB)
                    dve.wait_ge(bn_sq, 1)
                    v.tensor_scalar(bn[:, 1, :], psS[:, D:2 * D], 1.0 / N, 1.0 / N, ALU.mult, ALU.mult).then_inc(bn_var, 1)
                    dve.wait_ge(bn_std, 1)
                    link(v.reciprocal(bn[:, 1, :], bn[:, 2, :]))
                    link(v.scalar_tensor_tensor(bn[:, 1, :], bn[:, 1, :], float(N) ** -0.5, rowb[:, BGAM, :], ALU.mult, ALU.mult))
                    for b in range(NB):
                        at = slice(BT * b, BT * (b + 1))
                        link(v.tensor_tensor(hbn[:, at, :], hbn[:, at, :], over_tiles(bn[:, 1, :], BT), ALU.mult))
                        link(v.tensor_tensor(xt[:, at, :], xt[:, at, :], hbn[:, at, :], ALU.add))
                        moments(b)
                if next_normed:
                    for b in range(NB):
                        normalize(NORMED.index(p.number + 1), b)


_INS = ["x", "src", "dst", "L0_gnn_W", "L0_gnn_b", "L1_gnn_Ws", "L1_gnn_Wd", "L1_gnn_att_s", "L1_gnn_att_d", "L1_gnn_b",
        "L2_gnn_M_w", "L2_gnn_M_b", "L2_gnn_U_w", "L2_gnn_U_b", "L2_gnn_bn_gamma", "L2_gnn_bn_beta",
        "L3_gnn_W1_neigh", "L3_gnn_W1_root", "L3_gnn_b1", "L3_gnn_W2_neigh", "L3_gnn_W2_root", "L3_gnn_b2"]


def kernel(**inputs):
    import numpy as _np
    import concourse.bacc as _bacc
    from concourse import mybir as _mybir
    from concourse.bass_utils import run_bass_kernel_spmd as _run

    nc = _bacc.Bacc("TRN2", target_bir_lowering=False, num_devices=1)
    arrays, args = {}, []
    for name in _INS:
        a = _np.ascontiguousarray(inputs[name])
        arrays[f"in_{name}_dram"] = a
        args.append(nc.dram_tensor(f"in_{name}_dram", a.shape, _mybir.dt.from_np(a.dtype), kind="ExternalInput").ap())
    x = inputs["x"]
    args.append(nc.dram_tensor("out_0_dram", tuple(x.shape), _mybir.dt.float32, kind="ExternalOutput").ap())
    build(nc, *args)
    r = _run(nc, [arrays], core_ids=[0])
    return r.results[0]["out_0_dram"]
```
